# Optimizing a Trainium2 kernel written in Bass

```python
import numpy as np
import jax
import jax.numpy as jnp

def _softmax(x, axis=-1):
    return jax.nn.softmax(x, axis=axis)

def _gelu(x):
    return jax.nn.gelu(x, approximate=True)

def _silu(x):
    return jax.nn.silu(x)

def _sigmoid(x):
    return jax.nn.sigmoid(x)

def _layernorm(x, axis=-1, eps=1e-05):
    m = jnp.mean(x, axis=axis, keepdims=True)
    v = jnp.var(x, axis=axis, keepdims=True)
    return (x - m) / jnp.sqrt(v + eps)

def _scatter_add(tgt, idx, src, axis=0):
    return tgt.at[idx].add(src)

def _segment_sum(src, seg, n):
    return jax.ops.segment_sum(src, seg, n)
kernel_name = 'mk_xattn_ffn_d1_seqx_r4_c04711'

def setup_inputs(seed: int=0):
    np.random.seed(seed)
    _w = jnp.asarray

    def _rec_inputs():
        import jax
        import jax.numpy as jnp
        _rk = jax.random.key(seed)
        x = -0.0003929 + 0.9999 * jax.random.normal(jax.random.fold_in(_rk, 1), (4, 512, 256), jnp.float32)
        _lenS = 512 - jax.random.randint(jax.random.fold_in(_rk, 7), (4,), 0, max(1, 512 // 4) + 1, jnp.int32)
        _lenS2 = 512 - jax.random.randint(jax.random.fold_in(_rk, 8), (4,), 0, max(1, 512 // 4) + 1, jnp.int32)
        _ctx_1024P = jax.random.normal(jax.random.fold_in(_rk, 11), (4, 16, 256), jnp.float32)
        _ctx_1024c = jax.random.dirichlet(jax.random.fold_in(_rk, 511), 0.3 * jnp.ones((16,), jnp.float32), (4, 512))
        _ctx_1024t = jnp.einsum('bsk,bkd->bsd', _ctx_1024c, _ctx_1024P)
        _ctx_1024t = _ctx_1024t * jax.lax.rsqrt(jnp.mean(jnp.square(_ctx_1024t)) + 1e-12) * 0.953939
        ctx_1024 = 2.81802e-05 + 1.00001 * (_ctx_1024t + 0.3 * jax.random.normal(jax.random.fold_in(_rk, 611), (4, 512, 256), jnp.float32))
        return (x, ctx_1024)
    x, ctx_1024 = _rec_inputs()

    def _L0_xattn_setup():
        import math
        import jax, jax.numpy as jnp
        import numpy as np
        D_MODEL = 256
        N_HEADS = 16
        D_K = D_MODEL // N_HEADS

        def _autocorr_forward(queries, keys, values, Wq, bq, Wk, bk, Wv, bv, Wo, bo):
            B, L, D = queries.shape
            H, dk = (N_HEADS, D_K)
            q = (queries @ Wq.T + bq).reshape(B, L, H, dk)
            k = (keys @ Wk.T + bk).reshape(B, L, H, dk)
            v = (values @ Wv.T + bv).reshape(B, L, H, dk)
            qf = jnp.fft.rfft(q, axis=1)
            kf = jnp.fft.rfft(k, axis=1)
            corr = jnp.fft.irfft(qf * jnp.conj(kf), n=L, axis=1).mean(axis=-1)
            corr = corr.transpose(0, 2, 1)
            topk = min(max(1, int(math.log(L))), L)
            weights, delays = jax.lax.top_k(corr, topk)
            w = jax.nn.softmax(weights, axis=-1)
            idx = (jnp.arange(L)[None, None, None, :] - delays[..., None]) % L
            v_h = v.transpose(0, 2, 1, 3)
            gathered = jnp.take_along_axis(v_h[:, :, None], idx[..., None], axis=3)
            out = (w[..., None, None] * gathered).sum(axis=2)
            out = out.transpose(0, 2, 1, 3).reshape(B, L, D)
            return out @ Wo.T + bo
        key = jax.random.key(seed)
        ks = jax.random.split(key, 12)
        B, L, D = (8, 512, D_MODEL)
        scale = 1.0 / math.sqrt(D)
        inp = {'queries': jax.random.normal(ks[0], (B, L, D), jnp.float32), 'keys': jax.random.normal(ks[1], (B, L, D), jnp.float32), 'values': jax.random.normal(ks[2], (B, L, D), jnp.float32), 'Wq': jax.random.normal(ks[3], (D, D), jnp.float32) * scale, 'bq': jnp.zeros((D,), jnp.float32), 'Wk': jax.random.normal(ks[4], (D, D), jnp.float32) * scale, 'bk': jnp.zeros((D,), jnp.float32), 'Wv': jax.random.normal(ks[5], (D, D), jnp.float32) * scale, 'bv': jnp.zeros((D,), jnp.float32), 'Wo': jax.random.normal(ks[6], (D, D), jnp.float32) * scale, 'bo': jnp.zeros((D,), jnp.float32)}
        return inp
    _L0_xattn_all = _L0_xattn_setup()
    _L0_xattn_in = {k: v for k, v in _L0_xattn_all.items() if k in ('Wq', 'bq', 'Wk', 'bk', 'Wv', 'bv', 'Wo', 'bo')}
    del _L0_xattn_all

    def _L0_ffn_setup():
        import jax, jax.numpy as jnp
        import numpy as np
        EPS = 1e-05

        def rmsnorm(x):
            return x * jax.lax.rsqrt(jnp.mean(x * x, axis=-1, keepdims=True) + EPS)

        def act_quant(x):
            scale = 127.0 / jnp.clip(jnp.max(jnp.abs(x), axis=-1, keepdims=True), 1e-05)
            q = jnp.clip(jnp.round(x * scale), -128.0, 127.0) / scale
            return x + jax.lax.stop_gradient(q - x)

        def weight_quant(w):
            scale = 1.0 / jnp.clip(jnp.mean(jnp.abs(w)), 1e-05)
            q = jnp.clip(jnp.round(w * scale), -1.0, 1.0) / scale
            return w + jax.lax.stop_gradient(q - w)

        def bitlinear(x, w, b):
            xq = act_quant(rmsnorm(x))
            wq = weight_quant(w)
            return jnp.einsum('bsd,fd->bsf', xq, wq) + b
        key = jax.random.key(seed)
        k0, k1, k2 = jax.random.split(key, 3)
        B, S, D, F = (2, 2048, 256, 1024)
        x = jax.random.normal(k0, (B, S, D), dtype=jnp.float32)
        w1 = jax.random.normal(k1, (F, D), dtype=jnp.float32) * (1.0 / np.sqrt(D))
        b1 = jnp.zeros((F,), dtype=jnp.float32)
        w2 = jax.random.normal(k2, (D, F), dtype=jnp.float32) * (1.0 / np.sqrt(F))
        b2 = jnp.zeros((D,), dtype=jnp.float32)
        return {'x': x, 'w1': w1, 'b1': b1, 'w2': w2, 'b2': b2}
    _L0_ffn_all = _L0_ffn_setup()
    _L0_ffn_in = {k: v for k, v in _L0_ffn_all.items() if k in ('w1', 'b1', 'w2', 'b2')}
    del _L0_ffn_all
    return {'x': x, 'ctx_1024': ctx_1024, 'L0_xattn_Wq': _L0_xattn_in['Wq'], 'L0_xattn_bq': _L0_xattn_in['bq'], 'L0_xattn_Wk': _L0_xattn_in['Wk'], 'L0_xattn_bk': _L0_xattn_in['bk'], 'L0_xattn_Wv': _L0_xattn_in['Wv'], 'L0_xattn_bv': _L0_xattn_in['bv'], 'L0_xattn_Wo': _L0_xattn_in['Wo'], 'L0_xattn_bo': _L0_xattn_in['bo'], 'L0_ffn_w1': _L0_ffn_in['w1'], 'L0_ffn_b1': _L0_ffn_in['b1'], 'L0_ffn_w2': _L0_ffn_in['w2'], 'L0_ffn_b2': _L0_ffn_in['b2']}

def reference(x, ctx_1024, L0_xattn_Wq, L0_xattn_bq, L0_xattn_Wk, L0_xattn_bk, L0_xattn_Wv, L0_xattn_bv, L0_xattn_Wo, L0_xattn_bo, L0_ffn_w1, L0_ffn_b1, L0_ffn_w2, L0_ffn_b2):
    import jax
    import jax.numpy as jnp

    def _L0_xattn_ref(queries, keys, values, Wq, bq, Wk, bk, Wv, bv, Wo, bo):
        import math
        import jax, jax.numpy as jnp
        import numpy as np
        D_MODEL = 256
        N_HEADS = 16
        D_K = D_MODEL // N_HEADS

        def _autocorr_forward(queries, keys, values, Wq, bq, Wk, bk, Wv, bv, Wo, bo):
            B, L, D = queries.shape
            H, dk = (N_HEADS, D_K)
            q = (queries @ Wq.T + bq).reshape(B, L, H, dk)
            k = (keys @ Wk.T + bk).reshape(B, L, H, dk)
            v = (values @ Wv.T + bv).reshape(B, L, H, dk)
            qf = jnp.fft.rfft(q, axis=1)
            kf = jnp.fft.rfft(k, axis=1)
            corr = jnp.fft.irfft(qf * jnp.conj(kf), n=L, axis=1).mean(axis=-1)
            corr = corr.transpose(0, 2, 1)
            topk = min(max(1, int(math.log(L))), L)
            weights, delays = jax.lax.top_k(corr, topk)
            w = jax.nn.softmax(weights, axis=-1)
            idx = (jnp.arange(L)[None, None, None, :] - delays[..., None]) % L
            v_h = v.transpose(0, 2, 1, 3)
            gathered = jnp.take_along_axis(v_h[:, :, None], idx[..., None], axis=3)
            out = (w[..., None, None] * gathered).sum(axis=2)
            out = out.transpose(0, 2, 1, 3).reshape(B, L, D)
            return out @ Wo.T + bo
        return _autocorr_forward(queries, keys, values, Wq, bq, Wk, bk, Wv, bv, Wo, bo)

    def _L0_ffn_ref(x, w1, b1, w2, b2):
        import jax, jax.numpy as jnp
        import numpy as np
        EPS = 1e-05

        def rmsnorm(x):
            return x * jax.lax.rsqrt(jnp.mean(x * x, axis=-1, keepdims=True) + EPS)

        def act_quant(x):
            scale = 127.0 / jnp.clip(jnp.max(jnp.abs(x), axis=-1, keepdims=True), 1e-05)
            q = jnp.clip(jnp.round(x * scale), -128.0, 127.0) / scale
            return x + jax.lax.stop_gradient(q - x)

        def weight_quant(w):
            scale = 1.0 / jnp.clip(jnp.mean(jnp.abs(w)), 1e-05)
            q = jnp.clip(jnp.round(w * scale), -1.0, 1.0) / scale
            return w + jax.lax.stop_gradient(q - w)

        def bitlinear(x, w, b):
            xq = act_quant(rmsnorm(x))
            wq = weight_quant(w)
            return jnp.einsum('bsd,fd->bsf', xq, wq) + b
        h = bitlinear(x, w1, b1)
        h = jax.nn.gelu(h, approximate=False)
        return bitlinear(h, w2, b2)
    x = x + _L0_xattn_ref(_layernorm(x, axis=-1), ctx_1024, ctx_1024, L0_xattn_Wq, L0_xattn_bq, L0_xattn_Wk, L0_xattn_bk, L0_xattn_Wv, L0_xattn_bv, L0_xattn_Wo, L0_xattn_bo)
    x = x + _L0_ffn_ref(_layernorm(x, axis=-1), L0_ffn_w1, L0_ffn_b1, L0_ffn_w2, L0_ffn_b2)
    return x

_drawn_inputs = setup_inputs


def setup_inputs(seed=0):
    import zlib

    import numpy as np

    out = dict(_drawn_inputs(seed))
    spreads = {'L0_xattn_bq': (0.0, 0.1),
     'L0_xattn_bk': (0.0, 0.1),
     'L0_xattn_bv': (0.0, 0.1),
     'L0_xattn_bo': (0.0, 0.1),
     'L0_ffn_b1': (0.0, 0.1),
     'L0_ffn_b2': (0.0, 0.1)}
    factors = {}
    for name, (base, spread) in spreads.items():
        noise = np.random.default_rng([zlib.crc32(name.encode()), seed]).standard_normal(out[name].shape)
        drawn = base * np.exp(spread * noise) if base else spread * noise
        out[name] = jnp.asarray(drawn.astype(out[name].dtype))
    for name, factor in factors.items():
        out[name] = (out[name] * factor).astype(out[name].dtype)
    return out
```

```python
from contextlib import ExitStack

import numpy as np
import concourse.bass as bass
import concourse.mybir as mybir

F32 = mybir.dt.float32
BF16 = mybir.dt.bfloat16
ALU = mybir.AluOpType
ACT = mybir.ActivationFunctionType
AX = mybir.AxisListType

P = 128
NB, L, D = 4, 512, 256
H, DK = 16, 16
FF = 1024
NA = L // P
NC = D // P
NK = FF // P
TOPK = 6
RE_E, IM_E, RE_O, IM_O = range(4)
EPS = 1e-5
ROUND = 1.5 * 2.0 ** 23
ABSENT = -3.0e38
SLOT = {0: 0, 3: 1, 2: 2, 1: 3}


def dft_constants():
    theta = 2.0 * np.pi / L
    t = np.arange(P)
    m = np.arange(P // 2)
    even = np.concatenate([4 * m, 4 * m + 2])
    odd = 4 * np.arange(P) + 1

    def cos(f, n):
        return np.cos(theta * (np.multiply.outer(f, n) % L))

    def sin(f, n):
        return np.sin(theta * (np.multiply.outer(f, n) % L))

    im0 = -sin(t, even[:64])
    im0[:, 0] = np.cos(np.pi * t)
    forward = np.concatenate([cos(t, even[:64]), im0, cos(t, even[64:]), -sin(t, even[64:]),
                              cos(t, odd), -sin(t, odd), -sin(t, odd), -cos(t, odd)], axis=1)
    c = np.full((P, 1), 2.0 / L)
    c_even = c.copy()
    c_even[0] = 1.0 / L
    tau = np.arange(L)

    def im_even(n):
        rows = -c_even * sin(even, n)
        rows[0] = np.cos(np.pi * n) / L
        return rows

    to_corr = np.stack([c_even * cos(even, tau), im_even(tau), c * cos(odd, tau), -c * sin(odd, tau)], axis=1) / DK
    sign = np.where(np.arange(P) < 64, 1.0, -1.0)[:, None]
    to_out = np.stack([np.concatenate([c_even * cos(even, t), sign * c_even * cos(even, t)], axis=1),
                       np.concatenate([im_even(t), sign * im_even(t)], axis=1),
                       np.concatenate([c * cos(odd, t), c * sin(odd, t)], axis=1),
                       np.concatenate([-c * sin(odd, t), c * cos(odd, t)], axis=1)], axis=1)
    k = np.arange(P) % 32
    parts = np.stack([-np.isin(k, (1, 2, 4)).astype(float), -(k == 2).astype(float)], axis=1)
    return [np.ascontiguousarray(a, dtype=np.float32) for a in (forward, to_corr, to_out, np.eye(P), parts)]


def build(nc, x, ctx, wq_t, wkv_t, wo_t, bq, bkv, bo, w1_t, b1, w2_t, b2, c_forward, c_corr, c_out, c_eye, c_parts, out):
    es = ExitStack()
    with es:
        def sb(name, shape, dt=F32):
            return es.enter_context(nc.sbuf_tensor(name, shape, dt))

        def sem(name):
            return es.enter_context(nc.semaphore(name))

        forward = sb("forward", [P, 6 * P])
        to_corr = sb("to_corr", [P, 4, L])
        to_out = sb("to_out", [P, 4, 2 * P])
        eye = sb("eye", [P, P])
        eye16 = sb("eye16", [P, P], BF16)
        wq = sb("wq", [P, NC, D])
        wkv = sb("wkv", [P, NC, 2 * D])
        wo = sb("wo", [P, NC, D])
        w1q = sb("w1q", [P, NC, FF], BF16)
        w2q = sb("w2q", [P, NK, D], BF16)
        w1f = sb("w1f", [P, NC * FF])
        w2f = sb("w2f", [P, NC * FF])
        bq_row = sb("bq_row", [1, D])
        bkv_row = sb("bkv_row", [1, 2 * D])
        bkv_dc = sb("bkv_dc", [1, 2 * D])
        bo_all = sb("bo_all", [P, D])
        b1_all = sb("b1_all", [P, FF])
        b2_all = sb("b2_all", [P, D])
        res = sb("res", [P, NB, NA, D])
        ctx_in = sb("ctx_in", [P, 2, NA, D])
        stats = sb("stats", [P, NA, 6])
        mv = sb("mv", [P, NA, 2])
        rstd = sb("rstd", [P, NA])
        xn = sb("xn", [P, NA, D])
        x_sum = sb("x_sum", [P, 2, D])
        x_even = sb("x_even", [P, 2, D])
        x_odd = sb("x_odd", [P, 2, D])
        c_sum = sb("c_sum", [P, 2, D])
        c_even = sb("c_even", [P, 2, D])
        c_odd = sb("c_odd", [P, 2, D])
        x_f = sb("x_f", [P, NC, L])
        c_f = sb("c_f", [P, NC, L])
        kv_f = sb("kv_f", [P, NB, 4, 2 * D])
        prod = sb("prod", [P, 4, D])
        prod_sum = sb("prod_sum", [P, 2, 4, NB * H])
        cross = sb("cross", [P, 4, NB * H])
        corr = sb("corr", [NB * H, L + 2])
        rest = sb("rest", [NB * H, L + 2])
        top = sb("top", [NB * H, 8])
        neg_top = sb("neg_top", [NB * H, 1])
        expd = sb("expd", [NB * H, L])
        chosen = sb("chosen", [NB * H, L])
        gsum = sb("gsum", [NB * H, 1])
        grec = sb("grec", [NB * H, 1])
        g_t = sb("g_t", [P, NA, NB * H])
        g_sum = sb("g_sum", [P, 2, NB * H])
        g_even = sb("g_even", [P, 2, NB * H])
        g_odd = sb("g_odd", [P, 2, NB * H])
        g_re = sb("g_re", [P, 2, NB * H])
        g_im = sb("g_im", [P, 2, NB * H])
        g_rx = sb("g_rx", [P, 2, NB * H])
        out_f = sb("out_f", [P, 2, 2, D])
        m_a = sb("m_a", [P, 2, D])
        m_b = sb("m_b", [P, 2, D])
        m_c = sb("m_c", [P, 2, D])
        m_d = sb("m_d", [P, 2, D])
        pm = sb("pm", [P, 2 * P])
        out_t = sb("out_t", [P, NC, NA, P])
        var_all = sb("var_all", [P, NA])
        xc = sb("xc", [P, NA, D])
        xmax = sb("xmax", [P, NA])
        xr = sb("xr", [P, NA])
        xm = sb("xm", [P, NA])
        xscale = sb("xscale", [P, NA])
        xinv = sb("xinv", [P, NA])
        xv = sb("xv", [P, NA])
        xve = sb("xve", [P, NA])
        xr127 = sb("xr127", [P, NA])
        xdeq = sb("xdeq", [P, NA])
        xq = sb("xq", [P, NA, D], BF16)
        xq_t = sb("xq_t", [P, NA, NC, P], BF16)
        hid = w2f[:].rearrange("p (k f) -> p k f", k=2)
        b1_part = sb("b1_part", [P, FF], BF16)
        b1_rows = sb("b1_rows", [P, FF], BF16)
        parts = sb("parts", [P, 2])
        aug = sb("aug", [P, NA, 32], BF16)
        aug_t = sb("aug_t", [P, P], BF16)
        winv = sb("winv", [P, 1])
        s_part = sb("s_part", [P, NA])
        s_full = sb("s_full", [P, NA])
        hsquare = sb("hsquare", [P, FF])
        hss = sb("hss", [P, 2])
        hmax = sb("hmax", [P, 2])
        hr = sb("hr", [P, 2])
        hm = sb("hm", [P, 2])
        hms = sb("hms", [P, 2])
        hr127 = sb("hr127", [P, 2])
        hinv = sb("hinv", [P, 2])
        hscale = sb("hscale", [P, 2])
        hdeq = sb("hdeq", [P, 2])
        hq = sb("hq", [P, 2, FF], BF16)
        hq_t = sb("hq_t", [P, 2, NK, P], BF16)
        wsum = sb("wsum", [P, 2])
        wtot = sb("wtot", [P, 2])
        wmean = sb("wmean", [P, 2])
        wscale = sb("wscale", [P, 2])
        wdeq = sb("wdeq", [P, 2])
        half_neg = sb("half_neg", [P, NA])
        one_neg = sb("one_neg", [P, NA])
        eps = sb("eps", [P, 1])
        eps1 = sb("eps1", [P, NA])
        eps2 = sb("eps2", [P, NA])
        c127 = sb("c127", [P, NA])
        ones = sb("ones", [P, NA, 3])
        fence = sb("fence", [P, 1])

        psum = es.enter_context(nc.psum_tensor("psum", [P, 8, L], F32))

        def bank(i):
            return psum[:, i, :]
        K_BANKS, Q_BANKS, A_BANKS = 0, 4, 6
        H_BANKS, AT_BANK, Y_BANK, T_BANKS = 0, 4, 5, 6

        def t_bank(i):
            return bank(T_BANKS + i).bitcast(BF16)

        s = {}
        for name in ("c_fwd_in", "wq_in", "wkv_in", "bias_in", "late_in", "b1_in", "b1_step", "b1_made", "s_full_made", "s_hi_made", "s_part_made", "s_mid_made", "aug_made", "w1_in", "w2_in", "x_in0", "x_in1", "x_in2", "x_in3", "c_in0", "c_in1", "c_in2", "c_in3",
                     "consts", "stats_made", "mv_made", "rstd_t", "rstd_made", "xn_made", "x_sum_made", "xs_made",
                     "c_sum_made", "cs_made", "spec_done", "spec_copied", "q_done", "kv_done", "kv_copied",
                     "bkv_made", "kv_biased", "q_biased", "prod_made", "prod_used", "res_made",
                     "wabs_made", "wtot_made", "wmean_made", "wdeq_made", "wscale_made", "w_step", "w_quantised",
                     "cross_a", "cross_made", "corr_done", "corr_copied", "max_made", "neg_made", "sent_made",
                     "rest_made", "exp_made", "mask_made", "gsum_made", "grec_made", "g_made", "g_t_done", "g_t_copied",
                     "g_sum_made", "gs_made", "g_f_done", "g_f_copied", "g_ready",
                     "m_ab", "out_re_made", "m_cd", "out_im_made", "at_done", "pm_copied", "at_used",
                     "stats2_made", "mv2_made", "xc_made", "xmax_made", "xv_made", "xve_made", "xr_made", "xr127_made", "xm_made", "xinv_made", "xscale_made", "xround", "xq_made", "b2_added",
                     "xt_done", "xt_copied", "h_done", "hid_made", "hss_made", "hmax_made", "hms_made", "hr_made", "hr127_made", "hm_made", "hinv_made", "hdeq_made",
                     "hscale_made", "hround", "hq_made", "ht_done", "ht_copied", "y_done", "y_made",
                     "stored"):
            s[name] = sem(name)

        x_v = x.rearrange("b (a p) d -> p b a d", p=P)
        ctx_v = ctx.rearrange("b (a p) d -> p b a d", p=P)
        out_v = out.rearrange("b (a p) d -> p b a d", p=P)

        def by_heads(ap):
            return ap.rearrange("p f (h d) -> p f h d", d=DK)

        block = es.enter_context(nc.Block())

        @block.sync
        def _(sp):
            sp.dma_start(res[:, 0], x_v[:, 0]).then_inc(s["x_in0"], 16)
            sp.dma_start(forward[:], c_forward).then_inc(s["c_fwd_in"], 16)
            sp.dma_start(ctx_in[:, 0], ctx_v[:, 0]).then_inc(s["c_in0"], 16)
            sp.dma_start(wq[:], wq_t.rearrange("(c p) n -> p c n", p=P)).then_inc(s["wq_in"], 16)
            sp.dma_start(wkv[:], wkv_t.rearrange("(c p) n -> p c n", p=P)).then_inc(s["wkv_in"], 16)
            sp.dma_start(bq_row[:], bq.unsqueeze(0)).then_inc(s["bias_in"], 16)
            sp.dma_start(bkv_row[:], bkv.unsqueeze(0)).then_inc(s["bias_in"], 16)
            sp.dma_start(bo_all[:], bo.partition_broadcast(P)).then_inc(s["bias_in"], 16)
            sp.dma_start(res[:, 1], x_v[:, 1]).then_inc(s["x_in1"], 16)
            sp.dma_start(ctx_in[:, 1], ctx_v[:, 1]).then_inc(s["c_in1"], 16)
            sp.dma_start(res[:, 2], x_v[:, 2]).then_inc(s["x_in2"], 16)
            sp.dma_start(w1f[:].rearrange("p (c n) -> p c n", c=NC), w1_t.rearrange("(c p) n -> p c n", p=P)).then_inc(s["w1_in"], 16)
            sp.dma_start(w2f[:].rearrange("p (c n) -> p c n", c=NK), w2_t.rearrange("(c p) n -> p c n", p=P)).then_inc(s["w2_in"], 16)
            sp.dma_start(res[:, 3], x_v[:, 3]).then_inc(s["x_in3"], 16)
            sp.dma_start(b1_all[:], b1.partition_broadcast(P)).then_inc(s["b1_in"], 16)
            sp.dma_start(parts[:], c_parts).then_inc(s["b1_in"], 16)
            sp.dma_start(to_corr[:], c_corr).then_inc(s["late_in"], 16)
            sp.dma_start(eye[:], c_eye).then_inc(s["late_in"], 16)
            sp.dma_start(to_out[:], c_out).then_inc(s["late_in"], 16)
            sp.dma_start(wo[:], wo_t.rearrange("(c p) n -> p c n", p=P)).then_inc(s["late_in"], 16)
            sp.dma_start(b2_all[:], b2.partition_broadcast(P)).then_inc(s["late_in"], 16)
            for n in (2, 3):
                sp.wait_ge(s["cs_made"], n - 1)
                sp.dma_start(ctx_in[:, n % 2], ctx_v[:, n]).then_inc(s[f"c_in{n}"], 16)
            with sp.Fori(0, NB) as m:
                for j in range(NA):
                    sp.wait_ge(s["y_made"], m * NA + (j + 1))
                    sp.dma_start(out_v[:, m, j], res[:, m, j]).then_inc(s["stored"], 16)
            sp.wait_ge(s["stored"], 16 * NA * NB)

        LATE = 5 * 16

        @block.tensor
        def _(pe):
            def spectrum(dst, even, odd, c, done):
                cols = slice(c * P, (c + 1) * P)
                parts = dst.rearrange("q (k f) -> q k f", k=4)
                pe.matmul(parts[:, 0:2, 0:64], even[:, 0, cols], forward[:, 0:128].rearrange("p (k f) -> p k f", k=2),
                          start=True, stop=False)
                pe.matmul(parts[:, 0:2, 64:128], even[:, 1, cols], forward[:, 128:256].rearrange("p (k f) -> p k f", k=2),
                          start=False, stop=False)
                pe.matmul(dst[:, 256:512], odd[:, 0, cols], forward[:, 256:512], start=False, stop=False)
                pe.matmul(dst[:, 256:512], odd[:, 1, cols], forward[:, 512:768], start=False, stop=True).then_inc(done, 1)

            pe.wait_ge(s["c_fwd_in"], 16)
            def transform(n, first):
                for k, (even, odd, made) in enumerate(((x_even, x_odd, s["xs_made"]), (c_even, c_odd, s["cs_made"]))):
                    pe.wait_ge(made, n + 1)
                    for c in range(NC):
                        if k or not first:
                            pe.wait_ge(s["spec_copied"], n * 4 + (2 * k - 1 + c if k else 0))
                        spectrum(bank(A_BANKS + c), even, odd, c, s["spec_done"])
                for fam in range(2):
                    if fam == 0:
                        pe.wait_ge(s["wq_in"], 16)
                        pe.wait_ge(s["spec_copied"], n * 4 + 2)
                        if not first:
                            pe.wait_ge(s["prod_used"], n * 2)
                    for part in range(2):
                        ft = 2 * fam + part
                        for c in range(NC):
                            mm = pe.matmul(psum[:, Q_BANKS + fam, part * D:(part + 1) * D], x_f[:, c, ft * P:(ft + 1) * P],
                                           wq[:, c, :], start=(c == 0), stop=(c == NC - 1))
                    mm.then_inc(s["q_done"], 1)
                    if fam == 0:
                        pe.wait_ge(s["wkv_in"], 16)
                        pe.wait_ge(s["spec_copied"], n * 4 + 4)
                        if not first:
                            pe.wait_ge(s["kv_copied"], n * 4)
                    for part in range(2):
                        ft = 2 * fam + part
                        for c in range(NC):
                            mm = pe.matmul(bank(K_BANKS + ft), c_f[:, c, ft * P:(ft + 1) * P], wkv[:, c, :],
                                           start=(c == 0), stop=(c == NC - 1))
                        mm.then_inc(s["kv_done"], 1)

            transform(0, True)
            with pe.Fori(1, NB) as n:
                transform(n, False)

            pe.wait_ge(s["cross_made"], 4)
            pe.wait_ge(s["late_in"], LATE)
            pe.wait_ge(s["spec_copied"], 4 * NB)
            for ft in range(4):
                mm = pe.matmul(psum[0:NB * H, A_BANKS, :], cross[:, ft, :], to_corr[:, ft, :], start=(ft == 0), stop=(ft == 3))
            mm.then_inc(s["corr_done"], 1)
            pe.wait_ge(s["g_made"], 1)
            for a in range(NA):
                mm = pe.transpose(psum[:, A_BANKS + 1, a * 64:(a + 1) * 64], chosen[:, a * P:(a + 1) * P], eye[0:NB * H, 0:NB * H])
            mm.then_inc(s["g_t_done"], 1)
            pe.wait_ge(s["gs_made"], 2)
            gf = bank(A_BANKS).rearrange("p (k n) -> p k n", k=8)
            for part in range(2):
                pe.matmul(gf[0:64, part, :], forward[:, part * 64:(part + 1) * 64], g_even[:, 0, :], start=True, stop=True)
                pe.matmul(gf[64:128, part, :], forward[:, 128 + part * 64:128 + (part + 1) * 64], g_even[:, 1, :], start=True, stop=True)
            for part in range(2):
                pe.matmul(gf[:, 2 + part, :], forward[:, 256 + part * P:256 + (part + 1) * P], g_odd[:, 0, :], start=True, stop=False)
                mm = pe.matmul(gf[:, 2 + part, :], forward[:, 512 + part * P:512 + (part + 1) * P], g_odd[:, 1, :], start=False, stop=True)
            mm.then_inc(s["g_f_done"], 1)

            def inverse(n, c, first):
                if c == 0:
                    pe.wait_ge(s["out_re_made"], n + 1)
                    pe.wait_ge(s["out_im_made"], n + 1)
                if c or not first:
                    pe.wait_ge(s["at_used"], n * 4 + c)
                for ft in range(4):
                    fam, part = divmod(ft, 2)
                    mm = pe.matmul(psum[:, AT_BANK, fam * D:(fam + 1) * D], out_f[:, fam, part, c * P:(c + 1) * P],
                                   to_out[:, ft, :], start=(ft == 0), stop=(ft == 3))
                mm.then_inc(s["at_done"], 1)

            def project(n, half):
                pe.wait_ge(s["at_used"], n * 4 + (2 + half))
                for k in range(2):
                    a = 2 * half + k
                    for c in range(NC):
                        mm = pe.matmul(psum[:, AT_BANK, k * D:(k + 1) * D], out_t[:, c, SLOT[a], :], wo[:, c, :],
                                       start=(c == 0), stop=(c == NC - 1))
                mm.then_inc(s["at_done"], 1)

            def turn_x(m):
                pe.wait_ge(s["aug_made"], m + 1)
                pe.wait_ge(s["xq_made"], m + 1)
                t = t_bank(0).rearrange("p (a c r) -> p a c r", a=NA, c=NC)
                for a in range(NA):
                    for c in range(NC):
                        pe.transpose(t[:, a, c, :], xq[:, a, c * P:(c + 1) * P], eye16[:])
                pe.transpose(bank(AT_BANK).bitcast(BF16)[:, 0:P], aug[:].rearrange("p a k -> p (a k)"), eye16[:]).then_inc(s["xt_done"], 1)

            def up(m, j):
                if j == 0:
                    pe.wait_ge(s["xt_copied"], m * 2 + 2)
                if j >= 2:
                    pe.wait_ge(s["hid_made"], m * NA + (j - 1))
                for half in range(2):
                    cols = slice(half * L, (half + 1) * L)
                    dst = bank(H_BANKS + 2 * (j % 2) + half)
                    for c in range(NC):
                        pe.matmul(dst, xq_t[:, j, c, :], w1q[:, c, cols], start=(c == 0), stop=False)
                    mm = pe.matmul(dst, aug_t[32 * j:32 * j + 32, :], b1_rows[32 * j:32 * j + 32, cols], start=False, stop=True)
                mm.then_inc(s["h_done"], 1)

            def turn_h(m, j):
                pe.wait_ge(s["hq_made"], m * NA + (j + 1))
                for k in range(NK):
                    mm = pe.transpose(t_bank(j % 2)[:, k * P:(k + 1) * P], hq[:, j % 2, k * P:(k + 1) * P], eye16[:])
                mm.then_inc(s["ht_done"], 1)

            def down(m, j):
                pe.wait_ge(s["ht_copied"], m * NA + (j + 1))
                if j > 0:
                    pe.wait_ge(s["y_made"], m * NA + j)
                for k in range(NK):
                    mm = pe.matmul(psum[:, Y_BANK, (j % 2) * D:(j % 2 + 1) * D], hq_t[:, j % 2, k, :], w2q[:, k, :],
                                   start=(k == 0), stop=(k == NK - 1))
                mm.then_inc(s["y_done"], 1)

            def step(n, m):
                if m is not None:
                    up(m, 1)
                    turn_h(m, 0)
                if n is not None:
                    inverse(n, 0, m is None)
                if m is not None:
                    down(m, 0)
                if n is not None:
                    inverse(n, 1, m is None)
                if m is not None:
                    up(m, 2)
                    turn_h(m, 1)
                if n is not None:
                    project(n, 0)
                if m is not None:
                    down(m, 1)
                    up(m, 3)
                if n is not None:
                    project(n, 1)
                if m is not None:
                    turn_h(m, 2)
                    down(m, 2)
                    turn_h(m, 3)
                if n is not None:
                    turn_x(n)
                if m is not None:
                    down(m, 3)
                if n is not None:
                    up(n, 0)

            pe.wait_ge(s["g_f_copied"], 2)
            pe.wait_ge(s["consts"], 4)
            pe.wait_ge(s["w_quantised"], 2)
            pe.wait_ge(s["b1_made"], 1)
            step(0, None)
            with pe.Fori(1, NB) as n:
                step(n, n - 1)
            step(None, NB - 1)

        @block.scalar
        def _(act):
            with act.Fori(0, NB) as n:
                for k, dst in enumerate((x_f, c_f)):
                    for c in range(NC):
                        act.wait_ge(s["spec_done"], n * 4 + (2 * k + c + 1))
                        act.copy(dst[:, c, :], bank(A_BANKS + c)).then_inc(s["spec_copied"], 1)
                for ft in range(4):
                    act.wait_ge(s["kv_done"], n * 4 + (ft + 1))
                    act.copy(kv_f[:, n, ft, :], bank(K_BANKS + ft)).then_inc(s["kv_copied"], 1)

            act.wait_ge(s["neg_made"], 1)
            act.wait_ge(s["corr_copied"], 1)
            act.activation(expd[:], corr[:, 0:L], ACT.Exp, bias=neg_top[:, 0:1]).then_inc(s["exp_made"], 1)
            act.wait_ge(s["g_t_done"], 1)
            act.copy(g_t[:].rearrange("p a n -> p (a n)"), psum[:, A_BANKS + 1, 0:NA * 64]).then_inc(s["g_t_copied"], 1)

            def inverse_copy(n, c):
                act.wait_ge(s["at_done"], n * 4 + (c + 1))
                act.copy(pm[:], psum[:, AT_BANK, 0:2 * P]).then_inc(s["pm_copied"], 1)

            def gelu(m, j):
                if j == 0:
                    act.wait_ge(s["xscale_made"], m + 1)
                act.wait_ge(s["h_done"], m * NA + (j + 1))
                hb = psum[:, H_BANKS + 2 * (j % 2):H_BANKS + 2 * (j % 2) + 2, :].rearrange("p k n -> p (k n)")
                act.activation(hid[:, j % 2, :], hb, ACT.Gelu, scale=xdeq[:, j:j + 1]).then_inc(s["hid_made"], 1)
                act.wait_ge(s["hid_made"], m * NA + (j + 1))
                act.activation(hsquare[:], hid[:, j % 2, :], ACT.Square, scale=FF ** -0.5, accum_out=hss[:, j % 2:j % 2 + 1]).then_inc(s["hss_made"], 1)

            def copy_x(m):
                act.wait_ge(s["xt_done"], m + 1)
                act.copy(aug_t[:], bank(AT_BANK).bitcast(BF16)[:, 0:P]).then_inc(s["xt_copied"], 1)
                act.copy(xq_t[:].rearrange("p a c r -> p (a c r)"), t_bank(0)).then_inc(s["xt_copied"], 1)

            def copy_h(m, j):
                act.wait_ge(s["ht_done"], m * NA + (j + 1))
                act.copy(hq_t[:, j % 2].rearrange("p k r -> p (k r)"), t_bank(j % 2)).then_inc(s["ht_copied"], 1)

            def step(n, m):
                if m is not None:
                    gelu(m, 1)
                    copy_h(m, 0)
                if n is not None:
                    inverse_copy(n, 0)
                    inverse_copy(n, 1)
                if m is not None:
                    gelu(m, 2)
                    copy_h(m, 1)
                    gelu(m, 3)
                    copy_h(m, 2)
                    copy_h(m, 3)
                if n is not None:
                    copy_x(n)
                    gelu(n, 0)

            step(0, None)
            with act.Fori(1, NB) as n:
                step(n, n - 1)
            step(None, NB - 1)

        @block.vector
        def _(dve):
            def normalise(n):
                for a in range(NA):
                    ins = dve.bn_stats(stats[:, a, :], res[:, n, a, :])
                ins.then_inc(s["stats_made"], 1)
                dve.wait_ge(s["stats_made"], n + 1)
                for a in range(NA):
                    ins = dve.bn_aggr(mv[:, a, :], stats[:, a, :])
                ins.then_inc(s["mv_made"], 1)
                dve.wait_ge(s["rstd_made"], n + 1)
                for a in range(NA):
                    ins = dve.tensor_scalar(xn[:, a, :], res[:, n, a, :], mv[:, a, 0:1], rstd[:, a:a + 1], ALU.subtract, ALU.mult)
                ins.then_inc(s["xn_made"], 1)
                dve.wait_ge(s["xn_made"], n + 1)
                dve.tensor_tensor(x_sum[:], xn[:, 0:2, :], xn[:, 2:4, :], ALU.add).then_inc(s["x_sum_made"], 1)
                if n:
                    dve.wait_ge(s["spec_done"], n * 4)
                dve.tensor_tensor(x_odd[:], xn[:, 0:2, :], xn[:, 2:4, :], ALU.subtract)
                dve.wait_ge(s["x_sum_made"], n + 1)
                dve.tensor_tensor(x_even[:, 0, :], x_sum[:, 0, :], x_sum[:, 1, :], ALU.add)
                dve.tensor_tensor(x_even[:, 1, :], x_sum[:, 0, :], x_sum[:, 1, :], ALU.subtract).then_inc(s["xs_made"], 1)

            def multiply(n):
                for fam in range(2):
                    q = psum[:, Q_BANKS + fam, :].rearrange("p (k d) -> p k d", k=2)
                    k_re, k_im = kv_f[:, n, 2 * fam, 0:D], kv_f[:, n, 2 * fam + 1, 0:D]
                    dve.wait_ge(s["q_done"], n * 2 + (fam + 1))
                    if fam == 0:
                        dve.scalar_tensor_tensor(q[0:1, 0, :], bq_row[:], float(L), q[0:1, 0, :], ALU.mult, ALU.add).then_inc(s["q_biased"], 1)
                        dve.wait_ge(s["kv_biased"], n + 1)
                        dve.wait_ge(s["q_biased"], n + 1)
                    dve.wait_ge(s["kv_copied"], n * 4 + (2 * fam + 2))
                    dve.tensor_tensor(prod[:, 0:2, :], q, kv_f[:, n, 2 * fam:2 * fam + 2, 0:D], ALU.mult)
                    dve.tensor_tensor(prod[:, 2, :], q[:, 1, :], k_re, ALU.mult)
                    dve.tensor_tensor(prod[:, 3, :], q[:, 0, :], k_im, ALU.mult).then_inc(s["prod_made"], 1)
                    dve.wait_ge(s["prod_made"], n * 2 + (fam + 1))
                    dve.tensor_reduce(prod_sum[:, fam, :, bass.ds(n * H, H)], prod[:].rearrange("p k (h d) -> p k h d", d=DK),
                                      AX.X, ALU.add).then_inc(s["prod_used"], 1)
                    dve.wait_ge(s["prod_used"], n * 2 + (fam + 1))

            dve.memset(half_neg[:], -0.5)
            dve.memset(eps[:], EPS)
            dve.memset(eps1[:], 1.0 + EPS)
            dve.memset(eps2[:], EPS * EPS)
            dve.memset(c127[:], 127.0)
            dve.memset(ones[:], 1.0)
            dve.memset(one_neg[:], -1.0).then_inc(s["consts"], 1)
            dve.memset(aug[:], 0.0).then_inc(s["consts"], 1)
            dve.memset(corr[:, L:L + 2], ABSENT).then_inc(s["consts"], 1)
            dve.wait_ge(s["x_in0"], 16)
            normalise(0)
            dve.wait_ge(s["bias_in"], 48)
            dve.tensor_scalar(bkv_dc[:], bkv_row[:], float(L), None, ALU.mult).then_inc(s["bkv_made"], 1)
            dve.wait_ge(s["x_in1"], 16)
            normalise(1)
            multiply(0)
            dve.wait_ge(s["x_in2"], 16)
            normalise(2)
            multiply(1)
            dve.wait_ge(s["x_in3"], 16)
            for k, (w, arrived) in enumerate(((w1f, s["w1_in"]), (w2f, s["w2_in"]))):
                dve.wait_ge(arrived, 16)
                dve.tensor_reduce(wsum[:, k:k + 1], w[:], AX.X, ALU.add, apply_absolute_value=True).then_inc(s["wabs_made"], 1)
            normalise(3)
            multiply(2)
            dve.wait_ge(s["wtot_made"], 1)
            dve.tensor_scalar(wmean[:], wtot[:], 1.0 / (D * FF), 1e-5, ALU.mult, ALU.max).then_inc(s["wmean_made"], 1)
            dve.wait_ge(s["wmean_made"], 1)
            dve.tensor_scalar(wdeq[:], wmean[:], 1.0 / 127.0, None, ALU.mult).then_inc(s["wdeq_made"], 1)
            dve.wait_ge(s["wdeq_made"], 1)
            dve.reciprocal(winv[:], wdeq[:, 0:1])
            dve.reciprocal(wscale[:], wmean[:]).then_inc(s["wscale_made"], 1)
            dve.wait_ge(s["wscale_made"], 1)
            for k, (w, wq_) in enumerate(((w1f, w1q), (w2f, w2q))):
                dve.tensor_scalar(w[:], w[:], wscale[:, k:k + 1], 1.0, ALU.mult, ALU.min).then_inc(s["w_step"], 1)
            for k, (w, wq_) in enumerate(((w1f, w1q), (w2f, w2q))):
                dve.wait_ge(s["w_step"], 1 + k)
                dve.tensor_scalar(w[:], w[:], -1.0, ROUND, ALU.max, ALU.add).then_inc(s["w_step"], 1)
            for k, (w, wq_) in enumerate(((w1f, w1q), (w2f, w2q))):
                dve.wait_ge(s["w_step"], 3 + k)
                dve.tensor_scalar(wq_[:].rearrange("p c n -> p (c n)"), w[:], ROUND, None, ALU.subtract).then_inc(s["w_quantised"], 1)
            dve.wait_ge(s["b1_in"], 32)
            dve.tensor_copy(b1_part[:], b1_all[:]).then_inc(s["b1_step"], 1)
            dve.wait_ge(s["b1_step"], 1)
            dve.scalar_tensor_tensor(b1_all[:], b1_part[:], parts[:, 0:1], b1_all[:], ALU.mult, ALU.add).then_inc(s["b1_step"], 1)
            dve.wait_ge(s["b1_step"], 2)
            dve.tensor_copy(b1_part[:], b1_all[:]).then_inc(s["b1_step"], 1)
            dve.wait_ge(s["b1_step"], 3)
            dve.scalar_tensor_tensor(b1_rows[:], b1_part[:], parts[:, 1:2], b1_all[:], ALU.mult, ALU.add).then_inc(s["b1_made"], 1)
            multiply(3)

            e_re, e_im = cross[:, RE_E:RE_O + 1:2, :], cross[:, IM_E:IM_O + 1:2, :]
            dve.tensor_tensor(e_re, prod_sum[:, :, 0, :], prod_sum[:, :, 1, :], ALU.add).then_inc(s["cross_made"], 1)
            dve.tensor_tensor(e_im, prod_sum[:, :, 2, :], prod_sum[:, :, 3, :], ALU.subtract).then_inc(s["cross_made"], 1)
            dve.wait_ge(s["cross_made"], 2)
            dve.tensor_copy(cross[0:1, RE_E, :], prod_sum[0:1, 0, 0, :]).then_inc(s["cross_made"], 1)
            dve.tensor_copy(cross[0:1, IM_E, :], prod_sum[0:1, 0, 1, :]).then_inc(s["cross_made"], 1)

            dve.wait_ge(s["late_in"], LATE)
            dve.tensor_copy(eye16[:], eye[:]).then_inc(s["consts"], 1)

            dve.wait_ge(s["corr_done"], 1)
            dve.tensor_copy(corr[:, 0:L], psum[0:NB * H, A_BANKS, :]).then_inc(s["corr_copied"], 1)
            dve.wait_ge(s["corr_copied"], 1)
            dve.max(top[:], corr[:, 0:L]).then_inc(s["max_made"], 1)
            dve.wait_ge(s["max_made"], 1)
            dve.tensor_scalar(neg_top[:], top[:, 0:1], -1.0, None, ALU.mult).then_inc(s["neg_made"], 1)
            dve.memset(top[:, TOPK:8], ABSENT).then_inc(s["sent_made"], 1)
            dve.wait_ge(s["sent_made"], 1)
            dve.match_replace(rest[:], top[:], corr[:], -1.0e38).then_inc(s["rest_made"], 1)
            dve.wait_ge(s["rest_made"], 1)
            dve.tensor_tensor(rest[:, 0:L], corr[:, 0:L], rest[:, 0:L], ALU.not_equal).then_inc(s["mask_made"], 1)
            dve.wait_ge(s["mask_made"], 1)
            dve.wait_ge(s["exp_made"], 1)
            dve.tensor_tensor_reduce(out=expd[:], in0=expd[:], in1=rest[:, 0:L], scale=1.0, scalar=0.0,
                                     op0=ALU.mult, op1=ALU.add, accum_out=gsum[:]).then_inc(s["gsum_made"], 1)
            dve.wait_ge(s["gsum_made"], 1)
            dve.reciprocal(grec[:], gsum[:]).then_inc(s["grec_made"], 1)
            dve.wait_ge(s["grec_made"], 1)
            dve.tensor_scalar(chosen[:], expd[:], grec[:, 0:1], None, ALU.mult).then_inc(s["g_made"], 1)

            dve.wait_ge(s["g_t_copied"], 1)
            dve.tensor_tensor(g_sum[:], g_t[:, 0:2, :], g_t[:, 2:4, :], ALU.add).then_inc(s["g_sum_made"], 1)
            dve.tensor_tensor(g_odd[:], g_t[:, 0:2, :], g_t[:, 2:4, :], ALU.subtract).then_inc(s["gs_made"], 1)
            dve.wait_ge(s["g_sum_made"], 1)
            dve.tensor_tensor(g_even[:, 0, :], g_sum[:, 0, :], g_sum[:, 1, :], ALU.add)
            dve.tensor_tensor(g_even[:, 1, :], g_sum[:, 0, :], g_sum[:, 1, :], ALU.subtract).then_inc(s["gs_made"], 1)
            dve.wait_ge(s["g_f_done"], 1)
            gf = bank(A_BANKS).rearrange("p (f k n) -> p f k n", f=4, k=2)
            dve.tensor_copy(g_re[:], gf[:, 0:2, 0, :]).then_inc(s["g_f_copied"], 1)
            dve.tensor_copy(g_im[:], gf[:, 0:2, 1, :]).then_inc(s["g_f_copied"], 1)
            dve.wait_ge(s["g_f_copied"], 2)
            dve.tensor_copy(g_rx[:], g_re[:]).then_inc(s["g_ready"], 1)
            dve.wait_ge(s["g_ready"], 1)
            dve.tensor_copy(g_rx[0:1, 0, :], g_im[0:1, 0, :]).then_inc(s["g_ready"], 1)
            dve.wait_ge(s["g_ready"], 2)
            dve.memset(g_im[0:1, 0, :], 0.0).then_inc(s["g_ready"], 1)
            dve.wait_ge(s["g_ready"], 3)

            def g_of(g, n):
                return g[:, :, bass.ds(n * H, H)].unsqueeze(3).broadcast_to([P, 2, H, DK])

            def v_of(n, part):
                return by_heads(kv_f[:, n, part:part + 3:2, D:2 * D])

            def out_re(n, first):
                dve.tensor_tensor(by_heads(m_a[:]), v_of(n, 0), g_of(g_re, n), ALU.mult)
                dve.tensor_tensor(by_heads(m_b[:]), v_of(n, 1), g_of(g_im, n), ALU.mult).then_inc(s["m_ab"], 1)
                dve.wait_ge(s["m_ab"], n + 1)
                if not first:
                    dve.wait_ge(s["at_done"], n * 4)
                dve.tensor_tensor(out_f[:, :, 0, :], m_a[:], m_b[:], ALU.subtract).then_inc(s["out_re_made"], 1)

            def inverse_out(n, c):
                dve.wait_ge(s["pm_copied"], n * 2 + (c + 1))
                odd = psum[:, AT_BANK, 2 * P:4 * P]
                dve.tensor_tensor(out_t[:, c, 0:2].rearrange("p a t -> p (a t)"), pm[:], odd, ALU.add)
                dve.tensor_tensor(out_t[:, c, 2:4].rearrange("p a t -> p (a t)"), pm[:], odd, ALU.subtract).then_inc(s["at_used"], 1)

            def add_residual(n, half):
                dve.wait_ge(s["at_done"], n * 4 + (3 + half))
                if half == 0:
                    dve.wait_ge(s["res_made"], n + 1)
                x1 = res[:, n, 2 * half:2 * half + 2, :].rearrange("p a d -> p (a d)")
                dve.tensor_tensor(x1, x1, bank(AT_BANK), ALU.add).then_inc(s["at_used"], 1)

            def stats2(n):
                dve.wait_ge(s["at_used"], n * 4 + 4)
                dve.memset(fence[:], 0.0)
                for a in range(NA):
                    ins = dve.bn_stats(stats[:, a, :], res[:, n, a, :])
                ins.then_inc(s["stats2_made"], 1)
                dve.wait_ge(s["stats2_made"], n + 1)
                dve.memset(fence[:], 0.0)
                for a in range(NA):
                    ins = dve.bn_aggr(mv[:, a, :], stats[:, a, :])
                ins.then_inc(s["mv2_made"], 1)
                dve.wait_ge(s["mv2_made"], n + 1)

            def centre(n):
                for a in range(NA):
                    ins = dve.tensor_scalar(xc[:, a, :], res[:, n, a, :], mv[:, a, 0:1], None, ALU.subtract)
                ins.then_inc(s["xc_made"], 1)
                dve.wait_ge(s["xc_made"], n + 1)
                dve.tensor_reduce(xmax[:], xc[:], AX.X, ALU.max, apply_absolute_value=True).then_inc(s["xmax_made"], 1)

            def quantise_x(n):
                dve.wait_ge(s["xscale_made"], n + 1)
                for a in range(NA):
                    ins = dve.tensor_scalar(xc[:, a, :], xc[:, a, :], xscale[:, a:a + 1], ROUND, ALU.mult, ALU.add)
                ins.then_inc(s["xround"], 1)
                dve.wait_ge(s["xround"], n + 1)
                dve.tensor_scalar(xq[:].rearrange("p a d -> p (a d)"), xc[:].rearrange("p a d -> p (a d)"), ROUND, None,
                                  ALU.subtract).then_inc(s["xq_made"], 1)

            def hidden_max(m, j):
                dve.wait_ge(s["hid_made"], m * NA + (j + 1))
                dve.tensor_reduce(hmax[:, j % 2:j % 2 + 1], hid[:, j % 2, :], AX.X, ALU.max, apply_absolute_value=True).then_inc(s["hmax_made"], 1)

            def quantise_h(m, j):
                dve.wait_ge(s["hscale_made"], m * NA + (j + 1))
                p = j % 2
                dve.tensor_scalar(hid[:, p, :], hid[:, p, :], hscale[:, p:p + 1], ROUND, ALU.mult, ALU.add).then_inc(s["hround"], 1)
                dve.wait_ge(s["hround"], m * NA + (j + 1))
                dve.tensor_scalar(hq[:, p, :], hid[:, p, :], ROUND, None, ALU.subtract).then_inc(s["hq_made"], 1)

            def finish(m, j):
                dve.wait_ge(s["y_done"], m * NA + (j + 1))
                dve.wait_ge(s["hdeq_made"], m * NA + (j + 1))
                if j == 0:
                    dve.wait_ge(s["b2_added"], m + 1)
                dve.scalar_tensor_tensor(res[:, m, j, :], psum[:, Y_BANK, (j % 2) * D:(j % 2 + 1) * D], hdeq[:, j % 2:j % 2 + 1],
                                         res[:, m, j, :], ALU.mult, ALU.add).then_inc(s["y_made"], 1)

            def step(n, m):
                if m is not None:
                    quantise_h(m, 0)
                if n is not None:
                    out_re(n, m is None)
                if m is not None:
                    hidden_max(m, 1)
                if n is not None:
                    inverse_out(n, 0)
                if m is not None:
                    quantise_h(m, 1)
                if n is not None:
                    inverse_out(n, 1)
                if m is not None:
                    hidden_max(m, 2)
                    finish(m, 0)
                if n is not None:
                    add_residual(n, 0)
                if m is not None:
                    quantise_h(m, 2)
                if n is not None:
                    add_residual(n, 1)
                    stats2(n)
                if m is not None:
                    hidden_max(m, 3)
                    finish(m, 1)
                if n is not None:
                    centre(n)
                if m is not None:
                    quantise_h(m, 3)
                    finish(m, 2)
                if n is not None:
                    quantise_x(n)
                if m is not None:
                    finish(m, 3)
                if n is not None:
                    hidden_max(n, 0)

            step(0, None)
            with dve.Fori(1, NB) as n:
                step(n, n - 1)
            step(None, NB - 1)

        @block.gpsimd
        def _(pool):
            def layer_rstd(n):
                pool.wait_ge(s["mv_made"], n + 1)
                pool.tensor_scalar(var_all[:], mv[:, :, 1], 1.0, EPS, ALU.mult, ALU.add).then_inc(s["rstd_t"], 1)
                pool.wait_ge(s["rstd_t"], n + 1)
                pool.tensor_tensor(rstd[:], var_all[:], half_neg[:], ALU.pow).then_inc(s["rstd_made"], 1)

            def combine(n, p):
                pool.tensor_tensor(c_sum[:], ctx_in[:, p, 0:2, :], ctx_in[:, p, 2:4, :], ALU.add).then_inc(s["c_sum_made"], 1)
                if n:
                    pool.wait_ge(s["spec_done"], n * 4)
                pool.tensor_tensor(c_odd[:], ctx_in[:, p, 0:2, :], ctx_in[:, p, 2:4, :], ALU.subtract)
                pool.wait_ge(s["c_sum_made"], n + 1)
                pool.tensor_tensor(c_even[:, 0, :], c_sum[:, 0, :], c_sum[:, 1, :], ALU.add)
                pool.tensor_tensor(c_even[:, 1, :], c_sum[:, 0, :], c_sum[:, 1, :], ALU.subtract).then_inc(s["cs_made"], 1)

            def bias_kv(n):
                pool.wait_ge(s["kv_copied"], n * 4 + 1)
                row = kv_f[0:1, n, RE_E, :]
                pool.tensor_tensor(row, row, bkv_dc[:], ALU.add).then_inc(s["kv_biased"], 1)

            def bias_res(n):
                pool.wait_ge(s["xn_made"], n + 1)
                pool.tensor_tensor(res[:, n], res[:, n], bo_all[:].unsqueeze(1).broadcast_to([P, NA, D]), ALU.add).then_inc(s["res_made"], 1)

            pool.wait_ge(s["consts"], 1)
            layer_rstd(0)
            pool.wait_ge(s["c_in0"], 16)
            combine(0, 0)
            for n in range(NB):
                if n + 1 < NB:
                    layer_rstd(n + 1)
                if n == 0:
                    pool.wait_ge(s["bkv_made"], 1)
                bias_kv(n)
                if n + 1 < NB:
                    pool.wait_ge(s[f"c_in{n + 1}"], 16)
                    combine(n + 1, (n + 1) % 2)
                if n == 2:
                    pool.wait_ge(s["wabs_made"], 2)
                    pool.partition_all_reduce(wtot[:], wsum[:], P, bass.bass_isa.ReduceOp.add).then_inc(s["wtot_made"], 1)
                bias_res(n)

            def g_of(g, n):
                return g[:, :, bass.ds(n * H, H)].unsqueeze(3).broadcast_to([P, 2, H, DK])

            def v_of(n, part):
                return by_heads(kv_f[:, n, part:part + 3:2, D:2 * D])

            def out_im(n, first):
                pool.tensor_tensor(by_heads(m_c[:]), v_of(n, 1), g_of(g_rx, n), ALU.mult)
                pool.tensor_tensor(by_heads(m_d[:]), v_of(n, 0), g_of(g_im, n), ALU.mult).then_inc(s["m_cd"], 1)
                pool.wait_ge(s["m_cd"], n + 1)
                if not first:
                    pool.wait_ge(s["at_done"], n * 4)
                pool.tensor_tensor(out_f[:, :, 1, :], m_c[:], m_d[:], ALU.add).then_inc(s["out_im_made"], 1)

            def h_math(m, j):
                p = slice(j % 2, j % 2 + 1)
                t = m * NA + j
                pool.wait_ge(s["hss_made"], t + 1)
                pool.tensor_tensor(hms[:, p], hss[:, p], eps[:, 0:1], ALU.add).then_inc(s["hms_made"], 1)
                pool.wait_ge(s["hms_made"], t + 1)
                pool.tensor_tensor(hr[:, p], hms[:, p], half_neg[:, 0:1], ALU.pow).then_inc(s["hr_made"], 1)
                pool.wait_ge(s["hmax_made"], t + 1)
                pool.wait_ge(s["hr_made"], t + 1)
                pool.tensor_tensor(hr127[:, p], hr[:, p], c127[:, 0:1], ALU.mult).then_inc(s["hr127_made"], 1)
                pool.tensor_scalar(hm[:, p], hmax[:, p], hr[:, p], 1e-5, ALU.mult, ALU.max).then_inc(s["hm_made"], 1)
                pool.wait_ge(s["hm_made"], t + 1)
                pool.tensor_tensor(hinv[:, p], hm[:, p], one_neg[:, 0:1], ALU.pow).then_inc(s["hinv_made"], 1)
                pool.wait_ge(s["hr127_made"], t + 1)
                pool.wait_ge(s["hinv_made"], t + 1)
                pool.tensor_tensor(hscale[:, p], hinv[:, p], hr127[:, p], ALU.mult).then_inc(s["hscale_made"], 1)
                if j >= 2:
                    pool.wait_ge(s["y_made"], t - 1)
                pool.tensor_tensor(hdeq[:, p], hm[:, p], wdeq[:, 1:2], ALU.mult).then_inc(s["hdeq_made"], 1)

            def x_math(n, first):
                pool.wait_ge(s["mv2_made"], n + 1)
                pool.tensor_tensor(xv[:], mv[:, :, 1], eps1[:], ALU.mult).then_inc(s["xv_made"], 1)
                pool.wait_ge(s["xv_made"], n + 1)
                pool.tensor_tensor(xve[:], xv[:], eps2[:], ALU.add).then_inc(s["xve_made"], 1)
                pool.wait_ge(s["xve_made"], n + 1)
                pool.tensor_tensor(xr[:], xve[:], half_neg[:], ALU.pow).then_inc(s["xr_made"], 1)
                pool.wait_ge(s["xmax_made"], n + 1)
                pool.wait_ge(s["xr_made"], n + 1)
                pool.tensor_tensor(xr127[:], xr[:], c127[:], ALU.mult).then_inc(s["xr127_made"], 1)
                for a in range(NA):
                    ins = pool.tensor_scalar(xm[:, a:a + 1], xmax[:, a:a + 1], xr[:, a:a + 1], 1e-5, ALU.mult, ALU.max)
                ins.then_inc(s["xm_made"], 1)
                pool.wait_ge(s["xm_made"], n + 1)
                pool.tensor_tensor(xinv[:], xm[:], one_neg[:], ALU.pow).then_inc(s["xinv_made"], 1)
                if not first:
                    pool.wait_ge(s["hid_made"], n * NA)
                pool.wait_ge(s["xinv_made"], n + 1)
                pool.tensor_tensor(xdeq[:], xm[:], wdeq[:, 0:1].broadcast_to([P, NA]), ALU.mult)
                pool.wait_ge(s["xr127_made"], n + 1)
                pool.tensor_tensor(xscale[:], xinv[:], xr127[:], ALU.mult).then_inc(s["xscale_made"], 1)
                pool.tensor_tensor(s_full[:], xinv[:], winv[:].broadcast_to([P, NA]), ALU.mult).then_inc(s["s_full_made"], 1)
                if not first:
                    pool.wait_ge(s["xt_done"], n)
                pool.wait_ge(s["s_full_made"], n + 1)
                pool.tensor_tensor(aug[:, :, 0:3], s_full[:].unsqueeze(2).broadcast_to([P, NA, 3]), ones[:], ALU.mult).then_inc(s["s_hi_made"], 1)
                pool.wait_ge(s["s_hi_made"], n + 1)
                pool.tensor_tensor(s_part[:], s_full[:], aug[:, :, 0], ALU.subtract).then_inc(s["s_part_made"], 1)
                pool.wait_ge(s["s_part_made"], n + 1)
                pool.tensor_tensor(aug[:, :, 3:5], s_part[:].unsqueeze(2).broadcast_to([P, NA, 2]), ones[:, :, 0:2], ALU.mult).then_inc(s["s_mid_made"], 1)
                pool.wait_ge(s["s_mid_made"], n + 1)
                pool.tensor_tensor(aug[:, :, 5], s_part[:], aug[:, :, 3], ALU.subtract).then_inc(s["aug_made"], 1)

            def add_b2(m):
                pool.wait_ge(s["xq_made"], m + 1)
                pool.tensor_tensor(res[:, m], res[:, m], b2_all[:].unsqueeze(1).broadcast_to([P, NA, D]), ALU.add).then_inc(s["b2_added"], 1)

            def step(n, m):
                if n is not None:
                    out_im(n, m is None)
                if m is not None:
                    h_math(m, 1)
                    add_b2(m)
                    h_math(m, 2)
                    h_math(m, 3)
                if n is not None:
                    x_math(n, m is None)
                    h_math(n, 0)

            pool.wait_ge(s["late_in"], LATE)
            pool.wait_ge(s["w_quantised"], 2)
            pool.wait_ge(s["g_ready"], 3)
            step(0, None)
            with pool.Fori(1, NB) as n:
                step(n, n - 1)
            step(None, NB - 1)


def kernel(**inputs):
    import concourse.bacc as bacc
    from concourse.bass_utils import run_bass_kernel_spmd

    def given(name):
        return np.ascontiguousarray(inputs[name])

    def turned(name):
        return np.ascontiguousarray(np.asarray(inputs[name]).T)

    forward, to_corr, to_out, eye, parts = dft_constants()
    arrays = {
        "x": given("x"),
        "ctx": given("ctx_1024"),
        "wq_t": turned("L0_xattn_Wq"),
        "wkv_t": np.concatenate([turned("L0_xattn_Wk"), turned("L0_xattn_Wv")], axis=1),
        "wo_t": turned("L0_xattn_Wo"),
        "bq": given("L0_xattn_bq"),
        "bkv": np.concatenate([given("L0_xattn_bk"), given("L0_xattn_bv")]),
        "bo": given("L0_xattn_bo"),
        "w1_t": turned("L0_ffn_w1"),
        "b1": given("L0_ffn_b1"),
        "w2_t": turned("L0_ffn_w2"),
        "b2": given("L0_ffn_b2"),
        "c_forward": forward,
        "c_corr": to_corr,
        "c_out": to_out,
        "c_eye": eye,
        "c_parts": parts,
    }
    nc = bacc.Bacc("TRN2", target_bir_lowering=False, num_devices=1)
    args = [nc.dram_tensor(f"in_{k}", a.shape, mybir.dt.from_np(a.dtype), kind="ExternalInput").ap() for k, a in arrays.items()]
    out = nc.dram_tensor("out", (NB, L, D), F32, kind="ExternalOutput").ap()
    build(nc, *args, out)
    r = run_bass_kernel_spmd(nc, [{f"in_{k}": a for k, a in arrays.items()}], core_ids=[0])
    return r.results[0]["out"]
```

```python
from contextlib import ExitStack

import numpy as np
import concourse.bass as bass
import concourse.mybir as mybir

F32 = mybir.dt.float32
BF16 = mybir.dt.bfloat16
ALU = mybir.AluOpType
ACT = mybir.ActivationFunctionType
AX = mybir.AxisListType

P = 128
NB, L, D = 4, 512, 256
H, DK = 16, 16
FF = 1024
NA = L // P
NC = D // P
NK = FF // P
TOPK = 6
RE_E, IM_E, RE_O, IM_O = range(4)
NPART = 6
EPS = 1e-5
ROUND = 1.5 * 2.0 ** 23
ABSENT = -3.0e38
SLOT = {0: 0, 3: 1, 2: 2, 1: 3}


def dft_constants():
    theta = 2.0 * np.pi / L
    t = np.arange(P)
    m = np.arange(P // 2)
    even = np.concatenate([4 * m, 4 * m + 2])
    odd = 4 * np.arange(P) + 1

    def cos(f, n):
        return np.cos(theta * (np.multiply.outer(f, n) % L))

    def sin(f, n):
        return np.sin(theta * (np.multiply.outer(f, n) % L))

    im0 = -sin(t, even[:64])
    im0[:, 0] = np.cos(np.pi * t)
    forward = np.concatenate([cos(t, even[:64]), im0, cos(t, even[64:]), -sin(t, even[64:]),
                              cos(t, odd), -sin(t, odd), -sin(t, odd), -cos(t, odd)], axis=1)
    c = np.full((P, 1), 2.0 / L)
    c_even = c.copy()
    c_even[0] = 1.0 / L
    tau = np.arange(L)

    def im_even(n):
        rows = -c_even * sin(even, n)
        rows[0] = np.cos(np.pi * n) / L
        return rows

    to_corr = np.stack([c_even * cos(even, tau), im_even(tau), c * cos(odd, tau), -c * sin(odd, tau)], axis=1) / DK
    sign = np.where(np.arange(P) < 64, 1.0, -1.0)[:, None]
    to_out = np.stack([np.concatenate([c_even * cos(even, t), sign * c_even * cos(even, t)], axis=1),
                       np.concatenate([im_even(t), sign * im_even(t)], axis=1),
                       np.concatenate([c * cos(odd, t), c * sin(odd, t)], axis=1),
                       np.concatenate([-c * sin(odd, t), c * cos(odd, t)], axis=1)], axis=1)
    k = np.arange(NPART)
    parts = np.stack([-np.isin(k, (1, 2, 4)).astype(float), -(k == 2).astype(float)], axis=1)
    return [np.ascontiguousarray(a, dtype=np.float32) for a in (forward, to_corr, to_out, np.eye(P), parts)]


def build(nc, x, ctx, wq_t, wkv_t, wo_t, bq, bkv, bo, w1_t, b1, w2_t, b2, c_forward, c_corr, c_out, c_eye, c_parts, out):
    es = ExitStack()
    with es:
        def sb(name, shape, dt=F32):
            return es.enter_context(nc.sbuf_tensor(name, shape, dt))

        def sem(name):
            return es.enter_context(nc.semaphore(name))

        forward = sb("forward", [P, 6 * P])
        to_corr = sb("to_corr", [P, 4, L])
        to_out = sb("to_out", [P, 4, 2 * P])
        eye = sb("eye", [P, P])
        eye16 = sb("eye16", [P, P], BF16)
        wq = sb("wq", [P, NC, D])
        wkv = sb("wkv", [P, NC, 2 * D])
        wo = sb("wo", [P, NC, D])
        w1q = sb("w1q", [P, NC, FF], BF16)
        w2q = sb("w2q", [P, NK, D], BF16)
        w1f = sb("w1f", [P, NC * FF])
        w2f = sb("w2f", [P, NC * FF])
        bq_row = sb("bq_row", [1, D])
        bkv_row = sb("bkv_row", [1, 2 * D])
        bkv_dc = sb("bkv_dc", [1, 2 * D])
        bo_all = sb("bo_all", [P, D])
        b1_all = sb("b1_all", [NPART, FF])
        b2_all = sb("b2_all", [P, D])
        res = sb("res", [P, NB, NA, D])
        ctx_in = sb("ctx_in", [P, 2, NA, D])
        stats = sb("stats", [P, NA, 6])
        mv = sb("mv", [P, NA, 2])
        rstd = sb("rstd", [P, NA])
        xn = sb("xn", [P, NA, D])
        x_sum = sb("x_sum", [P, 2, D])
        x_even = sb("x_even", [P, 2, D])
        x_odd = sb("x_odd", [P, 2, D])
        c_sum = sb("c_sum", [P, 2, D])
        c_even = sb("c_even", [P, 2, D])
        c_odd = sb("c_odd", [P, 2, D])
        x_f = sb("x_f", [P, NC, L])
        c_f = sb("c_f", [P, NC, L])
        kv_f = sb("kv_f", [P, NB, 4, 2 * D])
        prod = sb("prod", [P, 4, D])
        prod_sum = sb("prod_sum", [P, 2, 4, NB * H])
        cross = sb("cross", [P, 4, NB * H])
        corr = sb("corr", [NB * H, L + 2])
        rest = sb("rest", [NB * H, L + 2])
        top = sb("top", [NB * H, 8])
        neg_top = sb("neg_top", [NB * H, 1])
        expd = sb("expd", [NB * H, L])
        chosen = sb("chosen", [NB * H, L])
        gsum = sb("gsum", [NB * H, 1])
        grec = sb("grec", [NB * H, 1])
        g_t = sb("g_t", [P, NA, NB * H])
        g_sum = sb("g_sum", [P, 2, NB * H])
        g_even = sb("g_even", [P, 2, NB * H])
        g_odd = sb("g_odd", [P, 2, NB * H])
        g_re = sb("g_re", [P, 2, NB * H])
        g_im = sb("g_im", [P, 2, NB * H])
        g_rx = sb("g_rx", [P, 2, NB * H])
        out_f = sb("out_f", [P, 2, 2, D])
        m_a = sb("m_a", [P, 2, D])
        m_b = sb("m_b", [P, 2, D])
        m_c = sb("m_c", [P, 2, D])
        m_d = sb("m_d", [P, 2, D])
        pm = sb("pm", [P, 2, 2 * P])
        out_t = sb("out_t", [P, NC, NA, P])
        var_all = sb("var_all", [P, NA])
        xc = sb("xc", [P, NA, D])
        xmax = sb("xmax", [P, NA])
        xr = sb("xr", [P, NA])
        xm = sb("xm", [P, NA])
        xscale = sb("xscale", [P, NA])
        xinv = sb("xinv", [P, NA])
        xv = sb("xv", [P, NA])
        xve = sb("xve", [P, NA])
        xr127 = sb("xr127", [P, NA])
        xround = c_f[:].rearrange("p c (k d) -> p (c k) d", k=2)
        xdeq = sb("xdeq", [P, NB, NA])
        xq = sb("xq", [P, NA, D], BF16)
        xq_t = sb("xq_t", [P, NB, NA, NC, P], BF16)
        hid = [w[:, k * FF:(k + 1) * FF] for w in (w1f, w2f) for k in range(2)]
        b1_part = sb("b1_part", [NPART, FF], BF16)
        b1_rows = sb("b1_rows", [NPART, FF], BF16)
        parts = sb("parts", [NPART, 2])
        aug = sb("aug", [P, NA, NPART], BF16)
        aug_t = sb("aug_t", [NPART, NB, NA, P], BF16)
        winv = sb("winv", [P, 1])
        s_part = sb("s_part", [P, NA])
        s_full = sb("s_full", [P, NA])
        hsquare = x_f[:].rearrange("p c n -> p (c n)")
        hss = sb("hss", [P, NA])
        hmax = sb("hmax", [P, NA])
        hr = sb("hr", [P, NA])
        hm = sb("hm", [P, NA])
        hms = sb("hms", [P, NA])
        hr127 = sb("hr127", [P, NA])
        hinv = sb("hinv", [P, NA])
        hscale = sb("hscale", [P, NA])
        hdeq = sb("hdeq", [P, NA])
        hq = sb("hq", [P, 2, FF], BF16)
        hq_t = sb("hq_t", [P, 2, NK, P], BF16)
        wsum = sb("wsum", [P, 2])
        wtot = sb("wtot", [P, 2])
        wmean = sb("wmean", [P, 2])
        wscale = sb("wscale", [P, 2])
        wdeq = sb("wdeq", [P, 2])
        half_neg = sb("half_neg", [P, NA])
        one_neg = sb("one_neg", [P, NA])
        eps = sb("eps", [P, 1])
        eps1 = sb("eps1", [P, NA])
        eps2 = sb("eps2", [P, NA])
        c127 = sb("c127", [P, NA])
        minus127 = sb("minus127", [P, NA])
        ones = sb("ones", [P, NA, 3])
        minus_round = sb("minus_round", [P, 1])
        fence = sb("fence", [P, 1])

        psum = es.enter_context(nc.psum_tensor("psum", [P, 8, L], F32))

        def bank(i):
            return psum[:, i, :]
        K_BANKS, Q_BANKS, A_BANKS = 0, 4, 6
        I_BANKS, O_BANKS = 0, 2
        H_BANKS, Y_BANKS, T_BANKS = 0, 4, 6

        def tile(m, j, back):
            return m - (back - j + NA - 1) // NA, (j - back) % NA, m * NA + (j - back)

        def t_bank(i):
            return bank(T_BANKS + i).bitcast(BF16)

        s = {}
        for name in ("c_fwd_in", "wq_in", "wkv_in", "bias_in", "late_in", "b1_in", "b1_step", "b1_made", "s_full_made", "s_hi_made", "s_part_made", "s_mid_made", "aug_made", "w1_in", "w2_in", "x_in0", "x_in1", "x_in2", "x_in3", "c_in0", "c_in1", "c_in2", "c_in3",
                     "consts", "stats_made", "mv_made", "rstd_t", "rstd_made", "xn_made", "x_sum_made", "xs_made",
                     "c_sum_made", "cs_made", "spec_done", "spec_copied", "q_done", "kv_done", "kv_copied",
                     "bkv_made", "kv_biased", "q_biased", "prod_made", "prod_used", "res_made",
                     "wabs_made", "wtot_made", "wmean_made", "wdeq_made", "wscale_made", "w_step", "w_quantised",
                     "cross_a", "cross_made", "corr_done", "corr_copied", "max_made", "neg_made", "sent_made",
                     "rest_made", "exp_made", "mask_made", "gsum_made", "grec_made", "g_made", "g_t_done", "g_t_copied",
                     "g_sum_made", "gs_made", "g_f_done", "g_f_copied", "g_ready",
                     "m_ab", "out_re_made", "m_cd", "out_im_made", "at_done", "pm_copied", "at_used",
                     "stats2_made", "mv2_made", "xc_made", "xmax_made", "xv_made", "xve_made", "xr_made", "xr127_made", "xm_made", "xinv_made", "xscale_made", "xround", "xq_made", "b2_added",
                     "xt_done", "xt_copied", "h_done", "hid_made", "hss_made", "hmax_made", "hms_made", "hr_made", "hr127_made", "hm_made", "hinv_made", "hdeq_made",
                     "hscale_made", "hround", "hq_made", "ht_done", "ht_copied", "y_done", "y_made",
                     "stored"):
            s[name] = sem(name)

        x_v = x.rearrange("b (a p) d -> p b a d", p=P)
        ctx_v = ctx.rearrange("b (a p) d -> p b a d", p=P)
        out_v = out.rearrange("b (a p) d -> p b a d", p=P)

        def by_heads(ap):
            return ap.rearrange("p f (h d) -> p f h d", d=DK)

        block = es.enter_context(nc.Block())

        @block.sync
        def _(sp):
            sp.dma_start(res[:, 0], x_v[:, 0]).then_inc(s["x_in0"], 16)
            sp.dma_start(forward[:], c_forward).then_inc(s["c_fwd_in"], 16)
            sp.dma_start(ctx_in[:, 0], ctx_v[:, 0]).then_inc(s["c_in0"], 16)
            sp.dma_start(wq[:], wq_t.rearrange("(c p) n -> p c n", p=P)).then_inc(s["wq_in"], 16)
            sp.dma_start(wkv[:], wkv_t.rearrange("(c p) n -> p c n", p=P)).then_inc(s["wkv_in"], 16)
            sp.dma_start(bq_row[:], bq.unsqueeze(0)).then_inc(s["bias_in"], 16)
            sp.dma_start(bkv_row[:], bkv.unsqueeze(0)).then_inc(s["bias_in"], 16)
            sp.dma_start(bo_all[:], bo.partition_broadcast(P)).then_inc(s["bias_in"], 16)
            sp.dma_start(res[:, 1], x_v[:, 1]).then_inc(s["x_in1"], 16)
            sp.dma_start(ctx_in[:, 1], ctx_v[:, 1]).then_inc(s["c_in1"], 16)
            sp.dma_start(res[:, 2], x_v[:, 2]).then_inc(s["x_in2"], 16)
            sp.dma_start(w1f[:].rearrange("p (c n) -> p c n", c=NC), w1_t.rearrange("(c p) n -> p c n", p=P)).then_inc(s["w1_in"], 16)
            sp.dma_start(w2f[:].rearrange("p (c n) -> p c n", c=NK), w2_t.rearrange("(c p) n -> p c n", p=P)).then_inc(s["w2_in"], 16)
            sp.dma_start(res[:, 3], x_v[:, 3]).then_inc(s["x_in3"], 16)
            sp.dma_start(b1_all[:], b1.partition_broadcast(NPART)).then_inc(s["b1_in"], 16)
            sp.dma_start(parts[:], c_parts).then_inc(s["b1_in"], 16)
            sp.dma_start(to_corr[:], c_corr).then_inc(s["late_in"], 16)
            sp.dma_start(eye[:], c_eye).then_inc(s["late_in"], 16)
            sp.dma_start(to_out[:], c_out).then_inc(s["late_in"], 16)
            sp.dma_start(wo[:], wo_t.rearrange("(c p) n -> p c n", p=P)).then_inc(s["late_in"], 16)
            sp.dma_start(b2_all[:], b2.partition_broadcast(P)).then_inc(s["late_in"], 16)
            for n in (2, 3):
                sp.wait_ge(s["cs_made"], n - 1)
                sp.dma_start(ctx_in[:, n % 2], ctx_v[:, n]).then_inc(s[f"c_in{n}"], 16)
            with sp.Fori(0, NB) as m:
                for j in range(NA):
                    sp.wait_ge(s["y_made"], m * NA + (j + 1))
                    sp.dma_start(out_v[:, m, j], res[:, m, j]).then_inc(s["stored"], 16)
            sp.wait_ge(s["stored"], 16 * NA * NB)

        LATE = 5 * 16

        @block.tensor
        def _(pe):
            def spectrum(dst, even, odd, c, done):
                cols = slice(c * P, (c + 1) * P)
                parts = dst.rearrange("q (k f) -> q k f", k=4)
                pe.matmul(parts[:, 0:2, 0:64], even[:, 0, cols], forward[:, 0:128].rearrange("p (k f) -> p k f", k=2),
                          start=True, stop=False)
                pe.matmul(parts[:, 0:2, 64:128], even[:, 1, cols], forward[:, 128:256].rearrange("p (k f) -> p k f", k=2),
                          start=False, stop=False)
                pe.matmul(dst[:, 256:512], odd[:, 0, cols], forward[:, 256:512], start=False, stop=False)
                pe.matmul(dst[:, 256:512], odd[:, 1, cols], forward[:, 512:768], start=False, stop=True).then_inc(done, 1)

            pe.wait_ge(s["c_fwd_in"], 16)
            def transform(n, first):
                for k, (even, odd, made) in enumerate(((x_even, x_odd, s["xs_made"]), (c_even, c_odd, s["cs_made"]))):
                    pe.wait_ge(made, n + 1)
                    for c in range(NC):
                        if k or not first:
                            pe.wait_ge(s["spec_copied"], n * 4 + (2 * k - 1 + c if k else 0))
                        spectrum(bank(A_BANKS + c), even, odd, c, s["spec_done"])
                for fam in range(2):
                    if fam == 0:
                        pe.wait_ge(s["wq_in"], 16)
                        pe.wait_ge(s["spec_copied"], n * 4 + 2)
                        if not first:
                            pe.wait_ge(s["prod_used"], n * 2)
                    for part in range(2):
                        ft = 2 * fam + part
                        for c in range(NC):
                            mm = pe.matmul(psum[:, Q_BANKS + fam, part * D:(part + 1) * D], x_f[:, c, ft * P:(ft + 1) * P],
                                           wq[:, c, :], start=(c == 0), stop=(c == NC - 1))
                    mm.then_inc(s["q_done"], 1)
                    if fam == 0:
                        pe.wait_ge(s["wkv_in"], 16)
                        pe.wait_ge(s["spec_copied"], n * 4 + 4)
                        if not first:
                            pe.wait_ge(s["kv_copied"], n * 4)
                    for part in range(2):
                        ft = 2 * fam + part
                        for c in range(NC):
                            mm = pe.matmul(bank(K_BANKS + ft), c_f[:, c, ft * P:(ft + 1) * P], wkv[:, c, :],
                                           start=(c == 0), stop=(c == NC - 1))
                        mm.then_inc(s["kv_done"], 1)

            transform(0, True)
            with pe.Fori(1, NB) as n:
                transform(n, False)

            pe.wait_ge(s["cross_made"], 4)
            pe.wait_ge(s["late_in"], LATE)
            pe.wait_ge(s["spec_copied"], 4 * NB)
            for ft in range(4):
                mm = pe.matmul(psum[0:NB * H, A_BANKS, :], cross[:, ft, :], to_corr[:, ft, :], start=(ft == 0), stop=(ft == 3))
            mm.then_inc(s["corr_done"], 1)
            pe.wait_ge(s["g_made"], 1)
            for a in range(NA):
                mm = pe.transpose(psum[:, A_BANKS + 1, a * 64:(a + 1) * 64], chosen[:, a * P:(a + 1) * P], eye[0:NB * H, 0:NB * H])
            mm.then_inc(s["g_t_done"], 1)
            pe.wait_ge(s["gs_made"], 2)
            gf = bank(A_BANKS).rearrange("p (k n) -> p k n", k=8)
            for part in range(2):
                pe.matmul(gf[0:64, part, :], forward[:, part * 64:(part + 1) * 64], g_even[:, 0, :], start=True, stop=True)
                pe.matmul(gf[64:128, part, :], forward[:, 128 + part * 64:128 + (part + 1) * 64], g_even[:, 1, :], start=True, stop=True)
            for part in range(2):
                pe.matmul(gf[:, 2 + part, :], forward[:, 256 + part * P:256 + (part + 1) * P], g_odd[:, 0, :], start=True, stop=False)
                mm = pe.matmul(gf[:, 2 + part, :], forward[:, 512 + part * P:512 + (part + 1) * P], g_odd[:, 1, :], start=False, stop=True)
            mm.then_inc(s["g_f_done"], 1)

            def inverse(n, c, first):
                if c == 0:
                    pe.wait_ge(s["out_re_made"], n + 1)
                    pe.wait_ge(s["out_im_made"], n + 1)
                if not first:
                    pe.wait_ge(s["at_used"], n * 4 + (c - 3))
                for ft in range(4):
                    fam, part = divmod(ft, 2)
                    mm = pe.matmul(psum[:, I_BANKS + c, fam * D:(fam + 1) * D], out_f[:, fam, part, c * P:(c + 1) * P],
                                   to_out[:, ft, :], start=(ft == 0), stop=(ft == 3))
                mm.then_inc(s["at_done"], 1)

            def project(n, half):
                if half == 0:
                    pe.wait_ge(s["at_used"], n * 4 + 2)
                for k in range(2):
                    a = 2 * half + k
                    for c in range(NC):
                        mm = pe.matmul(psum[:, O_BANKS + half, k * D:(k + 1) * D], out_t[:, c, SLOT[a], :], wo[:, c, :],
                                       start=(c == 0), stop=(c == NC - 1))
                mm.then_inc(s["at_done"], 1)

            def turn_x(n):
                pe.wait_ge(s["aug_made"], n + 1)
                pe.wait_ge(s["xq_made"], n + 1)
                t = t_bank(0).rearrange("p (a c r) -> p a c r", a=NA, c=NC)
                for a in range(NA):
                    for c in range(NC):
                        pe.transpose(t[:, a, c, :], xq[:, a, c * P:(c + 1) * P], eye16[:])
                for a in range(NA):
                    mm = pe.transpose(t_bank(1)[0:NPART, a * P:(a + 1) * P], aug[:, a, :], eye16[:])
                mm.then_inc(s["xt_done"], 1)

            def attend(n, first=False, last=False):
                project(n, 0)
                project(n, 1)
                if not last:
                    inverse(n + 1, 0, False)
                if not first:
                    turn_x(n - 1)
                if not last:
                    inverse(n + 1, 1, False)

            pe.wait_ge(s["g_f_copied"], 2)
            pe.wait_ge(s["consts"], 3)
            inverse(0, 0, True)
            inverse(0, 1, True)
            attend(0, first=True)
            with pe.Fori(1, NB - 1) as n:
                attend(n)
            attend(NB - 1, last=True)

            def up(m, j, first=False):
                _, _, t = tile(m, j, 0)
                if j == 0:
                    pe.wait_ge(s["xt_copied"], m * 2 + 2)
                if not first or j >= 2:
                    pe.wait_ge(s["hid_made"], t - 1)
                for half in range(2):
                    cols = slice(half * L, (half + 1) * L)
                    dst = bank(H_BANKS + 2 * (j % 2) + half)
                    for c in range(NC):
                        pe.matmul(dst, xq_t[:, m, j, c, :], w1q[:, c, cols], start=(c == 0), stop=False)
                    mm = pe.matmul(dst, aug_t[:, m, j, :], b1_rows[:, cols], start=False, stop=True)
                mm.then_inc(s["h_done"], 1)

            def turn_h(m, j, first=False):
                m, j, t = tile(m, j, 2)
                pe.wait_ge(s["hq_made"], t + 1)
                if not first or j >= 2:
                    pe.wait_ge(s["ht_copied"], t - 1)
                for k in range(NK):
                    mm = pe.transpose(t_bank(j % 2)[:, k * P:(k + 1) * P], hq[:, j % 2, k * P:(k + 1) * P], eye16[:])
                mm.then_inc(s["ht_done"], 1)

            def down(m, j):
                m, j, t = tile(m, j, 3)
                pe.wait_ge(s["ht_copied"], t + 1)
                for k in range(NK):
                    mm = pe.matmul(psum[:, Y_BANKS + j % 2, 0:D], hq_t[:, j % 2, k, :], w2q[:, k, :],
                                   start=(k == 0), stop=(k == NK - 1))
                mm.then_inc(s["y_done"], 1)

            pe.wait_ge(s["w_quantised"], 2)
            pe.wait_ge(s["b1_made"], 1)
            pe.wait_ge(s["at_used"], 4 * NB)
            up(0, 0, True)
            up(0, 1, True)
            turn_x(NB - 1)
            pe.wait_ge(s["xt_copied"], 2 * NB)
            up(0, 2, True)
            turn_h(0, 2, True)
            up(0, 3, True)
            down(0, 3)
            turn_h(0, 3, True)
            with pe.Fori(1, NB) as m:
                for j in range(NA):
                    up(m, j)
                    down(m, j)
                    turn_h(m, j)
            down(NB, 0)
            turn_h(NB, 0)
            down(NB, 1)
            turn_h(NB, 1)
            down(NB, 2)

        @block.scalar
        def _(act):
            with act.Fori(0, NB) as n:
                for k, dst in enumerate((x_f, c_f)):
                    for c in range(NC):
                        act.wait_ge(s["spec_done"], n * 4 + (2 * k + c + 1))
                        act.copy(dst[:, c, :], bank(A_BANKS + c)).then_inc(s["spec_copied"], 1)
                for ft in range(4):
                    act.wait_ge(s["kv_done"], n * 4 + (ft + 1))
                    act.copy(kv_f[:, n, ft, :], bank(K_BANKS + ft)).then_inc(s["kv_copied"], 1)

            act.wait_ge(s["neg_made"], 1)
            act.wait_ge(s["corr_copied"], 1)
            act.activation(expd[:], corr[:, 0:L], ACT.Exp, bias=neg_top[:, 0:1]).then_inc(s["exp_made"], 1)
            act.wait_ge(s["g_t_done"], 1)
            act.copy(g_t[:].rearrange("p a n -> p (a n)"), psum[:, A_BANKS + 1, 0:NA * 64]).then_inc(s["g_t_copied"], 1)

            def inverse_copy(n, c):
                act.wait_ge(s["at_done"], n * 4 + (c + 1))
                act.copy(pm[:, c], psum[:, I_BANKS + c, 0:2 * P]).then_inc(s["pm_copied"], 1)

            def centre(n, first):
                act.wait_ge(s["mv2_made"], n + 1)
                if not first:
                    act.wait_ge(s["xround"], n)
                for a in range(NA):
                    ins = act.activation(xc[:, a, :], res[:, n, a, :], ACT.Identity, bias=mv[:, a, 0:1], scale=-1.0)
                ins.then_inc(s["xc_made"], 1)

            def round_x(n):
                act.wait_ge(s["xround"], n + 1)
                act.activation(xq[:].rearrange("p a d -> p (a d)"), xround[:].rearrange("p a d -> p (a d)"), ACT.Identity,
                               bias=minus_round[:, 0:1]).then_inc(s["xq_made"], 1)

            def copy_x(n):
                act.wait_ge(s["xt_done"], n + 1)
                act.copy(aug_t[:, n].rearrange("k a r -> k (a r)"), t_bank(1)[0:NPART, 0:NA * P]).then_inc(s["xt_copied"], 1)
                act.copy(xq_t[:, n].rearrange("p a c r -> p (a c r)"), t_bank(0)).then_inc(s["xt_copied"], 1)

            def attend(n, first=False):
                inverse_copy(n, 0)
                inverse_copy(n, 1)
                if not first:
                    round_x(n - 1)
                centre(n, first)
                if not first:
                    copy_x(n - 1)

            attend(0, first=True)
            with act.Fori(1, NB) as n:
                attend(n)

            def gelu(m, j, first=False):
                _, _, t = tile(m, j, 0)
                act.wait_ge(s["h_done"], t + 1)
                if not first:
                    act.wait_ge(s["hq_made"], t - 3)
                hb = psum[:, H_BANKS + 2 * (j % 2):H_BANKS + 2 * (j % 2) + 2, :].rearrange("p k n -> p (k n)")
                act.activation(hid[j], hb, ACT.Gelu, scale=xdeq[:, m, j:j + 1]).then_inc(s["hid_made"], 1)
                act.wait_ge(s["hid_made"], t + 1)
                act.activation(hsquare, hid[j], ACT.Square, scale=FF ** -0.5, accum_out=hss[:, j:j + 1]).then_inc(s["hss_made"], 1)

            def copy_h(m, j, first=False):
                m, j, t = tile(m, j, 2)
                act.wait_ge(s["ht_done"], t + 1)
                if not first:
                    act.wait_ge(s["y_done"], t - 1)
                act.copy(hq_t[:, j % 2].rearrange("p k r -> p (k r)"), t_bank(j % 2)).then_inc(s["ht_copied"], 1)

            gelu(0, 0, True)
            round_x(NB - 1)
            copy_x(NB - 1)
            gelu(0, 1, True)
            gelu(0, 2, True)
            copy_h(0, 2, True)
            gelu(0, 3, True)
            copy_h(0, 3, True)
            with act.Fori(1, NB) as m:
                for j in range(NA):
                    gelu(m, j)
                    copy_h(m, j)
            copy_h(NB, 0)
            copy_h(NB, 1)

        @block.vector
        def _(dve):
            def normalise(n):
                for a in range(NA):
                    ins = dve.bn_stats(stats[:, a, :], res[:, n, a, :])
                ins.then_inc(s["stats_made"], 1)
                dve.wait_ge(s["stats_made"], n + 1)
                for a in range(NA):
                    ins = dve.bn_aggr(mv[:, a, :], stats[:, a, :])
                ins.then_inc(s["mv_made"], 1)
                dve.wait_ge(s["rstd_made"], n + 1)
                for a in range(NA):
                    ins = dve.tensor_scalar(xn[:, a, :], res[:, n, a, :], mv[:, a, 0:1], rstd[:, a:a + 1], ALU.subtract, ALU.mult)
                ins.then_inc(s["xn_made"], 1)
                dve.wait_ge(s["xn_made"], n + 1)
                dve.tensor_tensor(x_sum[:], xn[:, 0:2, :], xn[:, 2:4, :], ALU.add).then_inc(s["x_sum_made"], 1)
                if n:
                    dve.wait_ge(s["spec_done"], n * 4)
                dve.tensor_tensor(x_odd[:], xn[:, 0:2, :], xn[:, 2:4, :], ALU.subtract)
                dve.wait_ge(s["x_sum_made"], n + 1)
                dve.tensor_tensor(x_even[:, 0, :], x_sum[:, 0, :], x_sum[:, 1, :], ALU.add)
                dve.tensor_tensor(x_even[:, 1, :], x_sum[:, 0, :], x_sum[:, 1, :], ALU.subtract).then_inc(s["xs_made"], 1)

            def multiply(n):
                for fam in range(2):
                    q = psum[:, Q_BANKS + fam, :].rearrange("p (k d) -> p k d", k=2)
                    k_re, k_im = kv_f[:, n, 2 * fam, 0:D], kv_f[:, n, 2 * fam + 1, 0:D]
                    dve.wait_ge(s["q_done"], n * 2 + (fam + 1))
                    if fam == 0:
                        dve.scalar_tensor_tensor(q[0:1, 0, :], bq_row[:], float(L), q[0:1, 0, :], ALU.mult, ALU.add).then_inc(s["q_biased"], 1)
                        dve.wait_ge(s["kv_biased"], n + 1)
                        dve.wait_ge(s["q_biased"], n + 1)
                    dve.wait_ge(s["kv_copied"], n * 4 + (2 * fam + 2))
                    dve.tensor_tensor(prod[:, 0:2, :], q, kv_f[:, n, 2 * fam:2 * fam + 2, 0:D], ALU.mult)
                    dve.tensor_tensor(prod[:, 2, :], q[:, 1, :], k_re, ALU.mult)
                    dve.tensor_tensor(prod[:, 3, :], q[:, 0, :], k_im, ALU.mult).then_inc(s["prod_made"], 1)
                    dve.wait_ge(s["prod_made"], n * 2 + (fam + 1))
                    dve.tensor_reduce(prod_sum[:, fam, :, bass.ds(n * H, H)], prod[:].rearrange("p k (h d) -> p k h d", d=DK),
                                      AX.X, ALU.add).then_inc(s["prod_used"], 1)
                    dve.wait_ge(s["prod_used"], n * 2 + (fam + 1))

            dve.memset(half_neg[:], -0.5)
            dve.memset(eps[:], EPS)
            dve.memset(eps1[:], 1.0 + EPS)
            dve.memset(eps2[:], EPS * EPS)
            dve.memset(c127[:], 127.0)
            dve.memset(minus127[:], -127.0)
            dve.memset(minus_round[:], -ROUND)
            dve.memset(ones[:], 1.0)
            dve.memset(one_neg[:], -1.0).then_inc(s["consts"], 1)
            dve.memset(corr[:, L:L + 2], ABSENT).then_inc(s["consts"], 1)
            dve.wait_ge(s["x_in0"], 16)
            normalise(0)
            dve.wait_ge(s["bias_in"], 48)
            dve.tensor_scalar(bkv_dc[:], bkv_row[:], float(L), None, ALU.mult).then_inc(s["bkv_made"], 1)
            dve.wait_ge(s["x_in1"], 16)
            normalise(1)
            multiply(0)
            dve.wait_ge(s["x_in2"], 16)
            normalise(2)
            multiply(1)
            dve.wait_ge(s["x_in3"], 16)
            for k, (w, arrived) in enumerate(((w1f, s["w1_in"]), (w2f, s["w2_in"]))):
                dve.wait_ge(arrived, 16)
                dve.tensor_reduce(wsum[:, k:k + 1], w[:], AX.X, ALU.add, apply_absolute_value=True).then_inc(s["wabs_made"], 1)
            normalise(3)
            multiply(2)
            dve.wait_ge(s["wtot_made"], 1)
            dve.tensor_scalar(wmean[:], wtot[:], 1.0 / (D * FF), 1e-5, ALU.mult, ALU.max).then_inc(s["wmean_made"], 1)
            dve.wait_ge(s["wmean_made"], 1)
            dve.tensor_scalar(wdeq[:], wmean[:], 1.0 / 127.0, None, ALU.mult).then_inc(s["wdeq_made"], 1)
            dve.wait_ge(s["wdeq_made"], 1)
            dve.reciprocal(winv[:], wdeq[:, 0:1])
            dve.reciprocal(wscale[:], wmean[:]).then_inc(s["wscale_made"], 1)
            dve.wait_ge(s["wscale_made"], 1)
            for k, (w, wq_) in enumerate(((w1f, w1q), (w2f, w2q))):
                dve.tensor_scalar(w[:], w[:], wscale[:, k:k + 1], 1.0, ALU.mult, ALU.min).then_inc(s["w_step"], 1)
            for k, (w, wq_) in enumerate(((w1f, w1q), (w2f, w2q))):
                dve.wait_ge(s["w_step"], 1 + k)
                dve.tensor_scalar(w[:], w[:], -1.0, ROUND, ALU.max, ALU.add).then_inc(s["w_step"], 1)
            for k, (w, wq_) in enumerate(((w1f, w1q), (w2f, w2q))):
                dve.wait_ge(s["w_step"], 3 + k)
                dve.tensor_scalar(wq_[:].rearrange("p c n -> p (c n)"), w[:], ROUND, None, ALU.subtract).then_inc(s["w_quantised"], 1)
            dve.wait_ge(s["b1_in"], 32)
            dve.tensor_copy(b1_part[:], b1_all[:]).then_inc(s["b1_step"], 1)
            dve.wait_ge(s["b1_step"], 1)
            dve.scalar_tensor_tensor(b1_all[:], b1_part[:], parts[:, 0:1], b1_all[:], ALU.mult, ALU.add).then_inc(s["b1_step"], 1)
            dve.wait_ge(s["b1_step"], 2)
            dve.tensor_copy(b1_part[:], b1_all[:]).then_inc(s["b1_step"], 1)
            dve.wait_ge(s["b1_step"], 3)
            dve.scalar_tensor_tensor(b1_rows[:], b1_part[:], parts[:, 1:2], b1_all[:], ALU.mult, ALU.add).then_inc(s["b1_made"], 1)
            multiply(3)

            e_re, e_im = cross[:, RE_E:RE_O + 1:2, :], cross[:, IM_E:IM_O + 1:2, :]
            dve.tensor_tensor(e_re, prod_sum[:, :, 0, :], prod_sum[:, :, 1, :], ALU.add).then_inc(s["cross_made"], 1)
            dve.tensor_tensor(e_im, prod_sum[:, :, 2, :], prod_sum[:, :, 3, :], ALU.subtract).then_inc(s["cross_made"], 1)
            dve.wait_ge(s["cross_made"], 2)
            dve.tensor_copy(cross[0:1, RE_E, :], prod_sum[0:1, 0, 0, :]).then_inc(s["cross_made"], 1)
            dve.tensor_copy(cross[0:1, IM_E, :], prod_sum[0:1, 0, 1, :]).then_inc(s["cross_made"], 1)

            dve.wait_ge(s["late_in"], LATE)
            dve.tensor_copy(eye16[:], eye[:]).then_inc(s["consts"], 1)

            dve.wait_ge(s["corr_done"], 1)
            dve.tensor_copy(corr[:, 0:L], psum[0:NB * H, A_BANKS, :]).then_inc(s["corr_copied"], 1)
            dve.wait_ge(s["corr_copied"], 1)
            dve.max(top[:], corr[:, 0:L]).then_inc(s["max_made"], 1)
            dve.wait_ge(s["max_made"], 1)
            dve.tensor_scalar(neg_top[:], top[:, 0:1], -1.0, None, ALU.mult).then_inc(s["neg_made"], 1)
            dve.memset(top[:, TOPK:8], ABSENT).then_inc(s["sent_made"], 1)
            dve.wait_ge(s["sent_made"], 1)
            dve.match_replace(rest[:], top[:], corr[:], -1.0e38).then_inc(s["rest_made"], 1)
            dve.wait_ge(s["rest_made"], 1)
            dve.tensor_tensor(rest[:, 0:L], corr[:, 0:L], rest[:, 0:L], ALU.not_equal).then_inc(s["mask_made"], 1)
            dve.wait_ge(s["mask_made"], 1)
            dve.wait_ge(s["exp_made"], 1)
            dve.tensor_tensor_reduce(out=expd[:], in0=expd[:], in1=rest[:, 0:L], scale=1.0, scalar=0.0,
                                     op0=ALU.mult, op1=ALU.add, accum_out=gsum[:]).then_inc(s["gsum_made"], 1)
            dve.wait_ge(s["gsum_made"], 1)
            dve.reciprocal(grec[:], gsum[:]).then_inc(s["grec_made"], 1)
            dve.wait_ge(s["grec_made"], 1)
            dve.tensor_scalar(chosen[:], expd[:], grec[:, 0:1], None, ALU.mult).then_inc(s["g_made"], 1)

            dve.wait_ge(s["g_t_copied"], 1)
            dve.tensor_tensor(g_sum[:], g_t[:, 0:2, :], g_t[:, 2:4, :], ALU.add).then_inc(s["g_sum_made"], 1)
            dve.tensor_tensor(g_odd[:], g_t[:, 0:2, :], g_t[:, 2:4, :], ALU.subtract).then_inc(s["gs_made"], 1)
            dve.wait_ge(s["g_sum_made"], 1)
            dve.tensor_tensor(g_even[:, 0, :], g_sum[:, 0, :], g_sum[:, 1, :], ALU.add)
            dve.tensor_tensor(g_even[:, 1, :], g_sum[:, 0, :], g_sum[:, 1, :], ALU.subtract).then_inc(s["gs_made"], 1)
            dve.wait_ge(s["g_f_done"], 1)
            gf = bank(A_BANKS).rearrange("p (f k n) -> p f k n", f=4, k=2)
            dve.tensor_copy(g_re[:], gf[:, 0:2, 0, :]).then_inc(s["g_f_copied"], 1)
            dve.tensor_copy(g_im[:], gf[:, 0:2, 1, :]).then_inc(s["g_f_copied"], 1)
            dve.wait_ge(s["g_f_copied"], 2)
            dve.tensor_copy(g_rx[:], g_re[:]).then_inc(s["g_ready"], 1)
            dve.wait_ge(s["g_ready"], 1)
            dve.tensor_copy(g_rx[0:1, 0, :], g_im[0:1, 0, :]).then_inc(s["g_ready"], 1)
            dve.wait_ge(s["g_ready"], 2)
            dve.memset(g_im[0:1, 0, :], 0.0).then_inc(s["g_ready"], 1)
            dve.wait_ge(s["g_ready"], 3)

            def g_of(g, n):
                return g[:, :, bass.ds(n * H, H)].unsqueeze(3).broadcast_to([P, 2, H, DK])

            def v_of(n, part):
                return by_heads(kv_f[:, n, part:part + 3:2, D:2 * D])

            def out_re(n, first):
                dve.tensor_tensor(by_heads(m_a[:]), v_of(n, 0), g_of(g_re, n), ALU.mult)
                dve.tensor_tensor(by_heads(m_b[:]), v_of(n, 1), g_of(g_im, n), ALU.mult).then_inc(s["m_ab"], 1)
                dve.wait_ge(s["m_ab"], n + 1)
                if not first:
                    dve.wait_ge(s["at_done"], n * 4 - 2)
                dve.tensor_tensor(out_f[:, :, 0, :], m_a[:], m_b[:], ALU.subtract).then_inc(s["out_re_made"], 1)

            def inverse_out(n, c):
                dve.wait_ge(s["pm_copied"], n * 2 + (c + 1))
                odd = psum[:, I_BANKS + c, 2 * P:4 * P]
                dve.tensor_tensor(out_t[:, c, 0:2].rearrange("p a t -> p (a t)"), pm[:, c], odd, ALU.add)
                dve.tensor_tensor(out_t[:, c, 2:4].rearrange("p a t -> p (a t)"), pm[:, c], odd, ALU.subtract).then_inc(s["at_used"], 1)

            def add_residual(n, half):
                dve.wait_ge(s["at_done"], n * 4 + (3 + half))
                if half == 0:
                    dve.wait_ge(s["res_made"], n + 1)
                x1 = res[:, n, 2 * half:2 * half + 2, :].rearrange("p a d -> p (a d)")
                dve.tensor_tensor(x1, x1, bank(O_BANKS + half), ALU.add).then_inc(s["at_used"], 1)

            def stats2(n, first):
                dve.wait_ge(s["at_used"], n * 4 + 4)
                dve.memset(fence[:], 0.0)
                for a in range(NA):
                    ins = dve.bn_stats(stats[:, a, :], res[:, n, a, :])
                ins.then_inc(s["stats2_made"], 1)
                dve.wait_ge(s["stats2_made"], n + 1)
                if not first:
                    dve.wait_ge(s["xv_made"], n)
                dve.memset(fence[:], 0.0)
                for a in range(NA):
                    ins = dve.bn_aggr(mv[:, a, :], stats[:, a, :])
                ins.then_inc(s["mv2_made"], 1)

            def row_max(n):
                dve.wait_ge(s["xc_made"], n + 1)
                dve.tensor_reduce(xmax[:], xc[:], AX.X, ALU.max, apply_absolute_value=True).then_inc(s["xmax_made"], 1)

            def quantise_x(n):
                dve.wait_ge(s["xscale_made"], n + 1)
                for a in range(NA):
                    ins = dve.tensor_scalar(xround[:, a, :], xc[:, a, :], xscale[:, a:a + 1], ROUND, ALU.mult, ALU.add)
                ins.then_inc(s["xround"], 1)

            def attend(n, first=False, last=False):
                inverse_out(n, 0)
                inverse_out(n, 1)
                if not last:
                    out_re(n + 1, False)
                if not first:
                    row_max(n - 1)
                add_residual(n, 0)
                add_residual(n, 1)
                stats2(n, first)
                if not first:
                    quantise_x(n - 1)

            out_re(0, True)
            attend(0, first=True)
            with dve.Fori(1, NB - 1) as n:
                attend(n)
            attend(NB - 1, last=True)

            def hidden_max(m, j):
                _, _, t = tile(m, j, 0)
                dve.wait_ge(s["hid_made"], t + 1)
                dve.tensor_reduce(hmax[:, j:j + 1], hid[j], AX.X, ALU.max, apply_absolute_value=True).then_inc(s["hmax_made"], 1)

            def quantise_h(m, j, first=False):
                m, j, t = tile(m, j, 1)
                dve.wait_ge(s["hscale_made"], t + 1)
                dve.tensor_scalar(hid[j], hid[j], hscale[:, j:j + 1], ROUND, ALU.mult, ALU.add).then_inc(s["hround"], 1)
                dve.wait_ge(s["hround"], t + 1)
                if not first or j >= 2:
                    dve.wait_ge(s["ht_done"], t - 1)
                dve.tensor_scalar(hq[:, j % 2, :], hid[j], ROUND, None, ALU.subtract).then_inc(s["hq_made"], 1)

            def finish(m, j):
                m, j, t = tile(m, j, 3)
                dve.wait_ge(s["y_done"], t + 1)
                dve.wait_ge(s["hdeq_made"], t + 1)
                dve.wait_ge(s["b2_added"], t + 1)
                dve.scalar_tensor_tensor(res[:, m, j, :], psum[:, Y_BANKS + j % 2, 0:D], hdeq[:, j:j + 1],
                                         res[:, m, j, :], ALU.mult, ALU.add).then_inc(s["y_made"], 1)

            row_max(NB - 1)
            hidden_max(0, 0)
            quantise_x(NB - 1)
            hidden_max(0, 1)
            quantise_h(0, 1, True)
            hidden_max(0, 2)
            quantise_h(0, 2, True)
            finish(0, 3)
            hidden_max(0, 3)
            quantise_h(0, 3, True)
            with dve.Fori(1, NB) as m:
                for j in range(NA):
                    finish(m, j)
                    hidden_max(m, j)
                    quantise_h(m, j)
            finish(NB, 0)
            quantise_h(NB, 0)
            finish(NB, 1)
            finish(NB, 2)

        @block.gpsimd
        def _(pool):
            def layer_rstd(n):
                pool.wait_ge(s["mv_made"], n + 1)
                pool.tensor_scalar(var_all[:], mv[:, :, 1], 1.0, EPS, ALU.mult, ALU.add).then_inc(s["rstd_t"], 1)
                pool.wait_ge(s["rstd_t"], n + 1)
                pool.tensor_tensor(rstd[:], var_all[:], half_neg[:], ALU.pow).then_inc(s["rstd_made"], 1)

            def combine(n, p):
                pool.tensor_tensor(c_sum[:], ctx_in[:, p, 0:2, :], ctx_in[:, p, 2:4, :], ALU.add).then_inc(s["c_sum_made"], 1)
                if n:
                    pool.wait_ge(s["spec_done"], n * 4)
                pool.tensor_tensor(c_odd[:], ctx_in[:, p, 0:2, :], ctx_in[:, p, 2:4, :], ALU.subtract)
                pool.wait_ge(s["c_sum_made"], n + 1)
                pool.tensor_tensor(c_even[:, 0, :], c_sum[:, 0, :], c_sum[:, 1, :], ALU.add)
                pool.tensor_tensor(c_even[:, 1, :], c_sum[:, 0, :], c_sum[:, 1, :], ALU.subtract).then_inc(s["cs_made"], 1)

            def bias_kv(n):
                pool.wait_ge(s["kv_copied"], n * 4 + 1)
                row = kv_f[0:1, n, RE_E, :]
                pool.tensor_tensor(row, row, bkv_dc[:], ALU.add).then_inc(s["kv_biased"], 1)

            def bias_res(n):
                pool.wait_ge(s["xn_made"], n + 1)
                pool.tensor_tensor(res[:, n], res[:, n], bo_all[:].unsqueeze(1).broadcast_to([P, NA, D]), ALU.add).then_inc(s["res_made"], 1)

            pool.wait_ge(s["consts"], 1)
            layer_rstd(0)
            pool.wait_ge(s["c_in0"], 16)
            combine(0, 0)
            for n in range(NB):
                if n + 1 < NB:
                    layer_rstd(n + 1)
                if n == 0:
                    pool.wait_ge(s["bkv_made"], 1)
                bias_kv(n)
                if n + 1 < NB:
                    pool.wait_ge(s[f"c_in{n + 1}"], 16)
                    combine(n + 1, (n + 1) % 2)
                if n == 2:
                    pool.wait_ge(s["wabs_made"], 2)
                    pool.partition_all_reduce(wtot[:], wsum[:], P, bass.bass_isa.ReduceOp.add).then_inc(s["wtot_made"], 1)
                bias_res(n)

            def g_of(g, n):
                return g[:, :, bass.ds(n * H, H)].unsqueeze(3).broadcast_to([P, 2, H, DK])

            def v_of(n, part):
                return by_heads(kv_f[:, n, part:part + 3:2, D:2 * D])

            def out_im(n, first):
                if not first:
                    pool.wait_ge(s["out_im_made"], n)
                pool.tensor_tensor(by_heads(m_c[:]), v_of(n, 1), g_of(g_rx, n), ALU.mult)
                pool.tensor_tensor(by_heads(m_d[:]), v_of(n, 0), g_of(g_im, n), ALU.mult).then_inc(s["m_cd"], 1)
                pool.wait_ge(s["m_cd"], n + 1)
                if not first:
                    pool.wait_ge(s["at_done"], n * 4 - 2)
                pool.tensor_tensor(out_f[:, :, 1, :], m_c[:], m_d[:], ALU.add).then_inc(s["out_im_made"], 1)

            def h_math(m, j, first=False):
                p = slice(j, j + 1)
                _, _, t = tile(m, j, 0)
                pool.wait_ge(s["hss_made"], t + 1)
                pool.tensor_tensor(hms[:, p], hss[:, p], eps[:, 0:1], ALU.add).then_inc(s["hms_made"], 1)
                pool.wait_ge(s["hms_made"], t + 1)
                pool.tensor_tensor(hr[:, p], hms[:, p], half_neg[:, 0:1], ALU.pow).then_inc(s["hr_made"], 1)
                pool.wait_ge(s["hmax_made"], t + 1)
                pool.wait_ge(s["hr_made"], t + 1)
                pool.tensor_tensor(hr127[:, p], hr[:, p], c127[:, 0:1], ALU.mult).then_inc(s["hr127_made"], 1)
                pool.tensor_scalar(hm[:, p], hmax[:, p], hr[:, p], 1e-5, ALU.mult, ALU.max).then_inc(s["hm_made"], 1)
                pool.wait_ge(s["hm_made"], t + 1)
                pool.tensor_tensor(hinv[:, p], hm[:, p], one_neg[:, 0:1], ALU.pow).then_inc(s["hinv_made"], 1)
                pool.wait_ge(s["hr127_made"], t + 1)
                pool.wait_ge(s["hinv_made"], t + 1)
                pool.tensor_tensor(hscale[:, p], hinv[:, p], hr127[:, p], ALU.mult).then_inc(s["hscale_made"], 1)
                if not first:
                    pool.wait_ge(s["y_made"], t - 3)
                pool.tensor_tensor(hdeq[:, p], hm[:, p], wdeq[:, 1:2], ALU.mult).then_inc(s["hdeq_made"], 1)

            def x_math(n, first):
                pool.wait_ge(s["mv2_made"], n + 1)
                pool.tensor_tensor(xv[:], mv[:, :, 1], eps1[:], ALU.mult).then_inc(s["xv_made"], 1)
                pool.wait_ge(s["xv_made"], n + 1)
                pool.tensor_tensor(xve[:], xv[:], eps2[:], ALU.add).then_inc(s["xve_made"], 1)
                pool.wait_ge(s["xve_made"], n + 1)
                pool.tensor_tensor(xr[:], xve[:], half_neg[:], ALU.pow).then_inc(s["xr_made"], 1)
                pool.wait_ge(s["xmax_made"], n + 1)
                pool.wait_ge(s["xr_made"], n + 1)
                pool.tensor_tensor(xr127[:], xr[:], minus127[:], ALU.mult).then_inc(s["xr127_made"], 1)
                for a in range(NA):
                    ins = pool.tensor_scalar(xm[:, a:a + 1], xmax[:, a:a + 1], xr[:, a:a + 1], 1e-5, ALU.mult, ALU.max)
                ins.then_inc(s["xm_made"], 1)
                pool.wait_ge(s["xm_made"], n + 1)
                pool.tensor_tensor(xinv[:], xm[:], one_neg[:], ALU.pow).then_inc(s["xinv_made"], 1)
                pool.wait_ge(s["xinv_made"], n + 1)
                pool.tensor_tensor(xdeq[:, n], xm[:], wdeq[:, 0:1].broadcast_to([P, NA]), ALU.mult)
                pool.wait_ge(s["xr127_made"], n + 1)
                pool.tensor_tensor(xscale[:], xinv[:], xr127[:], ALU.mult).then_inc(s["xscale_made"], 1)
                pool.tensor_tensor(s_full[:], xinv[:], winv[:].broadcast_to([P, NA]), ALU.mult).then_inc(s["s_full_made"], 1)
                if not first:
                    pool.wait_ge(s["xt_done"], n)
                pool.wait_ge(s["s_full_made"], n + 1)
                pool.tensor_tensor(aug[:, :, 0:3], s_full[:].unsqueeze(2).broadcast_to([P, NA, 3]), ones[:], ALU.mult).then_inc(s["s_hi_made"], 1)
                pool.wait_ge(s["s_hi_made"], n + 1)
                pool.tensor_tensor(s_part[:], s_full[:], aug[:, :, 0], ALU.subtract).then_inc(s["s_part_made"], 1)
                pool.wait_ge(s["s_part_made"], n + 1)
                pool.tensor_tensor(aug[:, :, 3:5], s_part[:].unsqueeze(2).broadcast_to([P, NA, 2]), ones[:, :, 0:2], ALU.mult).then_inc(s["s_mid_made"], 1)
                pool.wait_ge(s["s_mid_made"], n + 1)
                pool.tensor_tensor(aug[:, :, 5], s_part[:], aug[:, :, 3], ALU.subtract).then_inc(s["aug_made"], 1)

            def add_b2(m, j):
                if j == 0:
                    pool.wait_ge(s["xc_made"], m + 1)
                pool.tensor_tensor(res[:, m, j, :], res[:, m, j, :], b2_all[:], ALU.add).then_inc(s["b2_added"], 1)

            pool.wait_ge(s["late_in"], LATE)
            pool.wait_ge(s["w_quantised"], 2)
            pool.wait_ge(s["g_ready"], 3)
            out_im(0, True)
            out_im(1, False)
            out_im(2, False)
            x_math(0, True)
            with pool.Fori(1, NB - 2) as n:
                out_im(n + 2, False)
                x_math(n, False)
            x_math(NB - 2, False)
            x_math(NB - 1, False)

            for j in range(NA):
                add_b2(0, j)
                h_math(0, j, True)
            with pool.Fori(1, NB) as m:
                for j in range(NA):
                    add_b2(m, j)
                    h_math(m, j)


def kernel(**inputs):
    import concourse.bacc as bacc
    from concourse.bass_utils import run_bass_kernel_spmd

    def given(name):
        return np.ascontiguousarray(inputs[name])

    def turned(name):
        return np.ascontiguousarray(np.asarray(inputs[name]).T)

    forward, to_corr, to_out, eye, parts = dft_constants()
    arrays = {
        "x": given("x"),
        "ctx": given("ctx_1024"),
        "wq_t": turned("L0_xattn_Wq"),
        "wkv_t": np.concatenate([turned("L0_xattn_Wk"), turned("L0_xattn_Wv")], axis=1),
        "wo_t": turned("L0_xattn_Wo"),
        "bq": given("L0_xattn_bq"),
        "bkv": np.concatenate([given("L0_xattn_bk"), given("L0_xattn_bv")]),
        "bo": given("L0_xattn_bo"),
        "w1_t": turned("L0_ffn_w1"),
        "b1": given("L0_ffn_b1"),
        "w2_t": turned("L0_ffn_w2"),
        "b2": given("L0_ffn_b2"),
        "c_forward": forward,
        "c_corr": to_corr,
        "c_out": to_out,
        "c_eye": eye,
        "c_parts": parts,
    }
    nc = bacc.Bacc("TRN2", target_bir_lowering=False, num_devices=1)
    args = [nc.dram_tensor(f"in_{k}", a.shape, mybir.dt.from_np(a.dtype), kind="ExternalInput").ap() for k, a in arrays.items()]
    out = nc.dram_tensor("out", (NB, L, D), F32, kind="ExternalOutput").ap()
    build(nc, *args, out)
    r = run_bass_kernel_spmd(nc, [{f"in_{k}": a for k, a in arrays.items()}], core_ids=[0])
    return r.results[0]["out"]
```

```python
from contextlib import ExitStack

import numpy as np
import concourse.bass as bass
import concourse.mybir as mybir

F32 = mybir.dt.float32
BF16 = mybir.dt.bfloat16
I16 = mybir.dt.int16
I32 = mybir.dt.int32
ALU = mybir.AluOpType
ACT = mybir.ActivationFunctionType
AX = mybir.AxisListType

P = 128
NB, L, D = 4, 512, 256
H, DK = 16, 16
FF = 1024
NA = L // P
NC = D // P
NK = FF // P
TOPK = 6
NG = 2
GR = NB // NG * H
RE_E, IM_E, RE_O, IM_O = range(4)
NPART = 6
EPS = 1e-5
ABSENT = -3.0e38
SLOT = {0: 0, 3: 1, 2: 2, 1: 3}


def dft_constants():
    theta = 2.0 * np.pi / L
    t = np.arange(P)
    m = np.arange(P // 2)
    even = np.concatenate([4 * m, 4 * m + 2])
    odd = 4 * np.arange(P) + 1

    def cos(f, n):
        return np.cos(theta * (np.multiply.outer(f, n) % L))

    def sin(f, n):
        return np.sin(theta * (np.multiply.outer(f, n) % L))

    im0 = -sin(t, even[:64])
    im0[:, 0] = np.cos(np.pi * t)
    forward = np.concatenate([cos(t, even[:64]), im0, cos(t, even[64:]), -sin(t, even[64:]),
                              cos(t, odd), -sin(t, odd), -sin(t, odd), -cos(t, odd)], axis=1)
    c = np.full((P, 1), 2.0 / L)
    c_even = c.copy()
    c_even[0] = 1.0 / L

    def im_even(n):
        rows = -c_even * sin(even, n)
        rows[0] = np.cos(np.pi * n) / L
        return rows

    sign = np.where(np.arange(P) < 64, 1.0, -1.0)[:, None]
    to_signal = np.stack([np.concatenate([c_even * cos(even, t), sign * c_even * cos(even, t)], axis=1),
                       np.concatenate([im_even(t), sign * im_even(t)], axis=1),
                       np.concatenate([c * cos(odd, t), c * sin(odd, t)], axis=1),
                       np.concatenate([-c * sin(odd, t), c * cos(odd, t)], axis=1)], axis=1)
    k = np.arange(NPART)
    parts = np.stack([-np.isin(k, (1, 2, 4)).astype(float), -(k == 2).astype(float)], axis=1)
    return [np.ascontiguousarray(a, dtype=np.float32) for a in (forward, to_signal, np.eye(P), parts)]


def build(nc, x, ctx, wq_t, wkv_t, wo_t, bq, bkv, bo, w1_t, b1, w2_t, b2, c_forward, c_signal, c_eye, c_parts, out):
    es = ExitStack()
    with es:
        def sb(name, shape, dt=F32):
            return es.enter_context(nc.sbuf_tensor(name, shape, dt))

        def sem(name):
            return es.enter_context(nc.semaphore(name))

        forward = sb("forward", [P, 6 * P])
        to_signal = sb("to_signal", [P, 4, 2 * P])
        eye = sb("eye", [P, P])
        eye16 = sb("eye16", [P, P], BF16)
        wq = sb("wq", [P, NC, D])
        wkv = sb("wkv", [P, NC, 2 * D])
        wo = sb("wo", [P, NC, D])
        w1q = sb("w1q", [P, NC, FF], BF16)
        w2q = sb("w2q", [P, NK, D], BF16)
        w1f = sb("w1f", [P, NC * FF])
        w2f = sb("w2f", [P, NC * FF])
        bq_row = sb("bq_row", [1, D])
        bkv_row = sb("bkv_row", [1, 2 * D])
        bkv_dc = sb("bkv_dc", [1, 2 * D])
        bo_all = sb("bo_all", [P, D])
        b1_all = sb("b1_all", [NPART, FF])
        b2_all = sb("b2_all", [P, D])
        res = sb("res", [P, NB, NA, D])
        ctx_in = sb("ctx_in", [P, 2, NA, D])
        stats = sb("stats", [P, NA, 6])
        mv = sb("mv", [P, NA, 2])
        rstd = sb("rstd", [P, NA])
        xn = sb("xn", [P, NA, D])
        x_sum = sb("x_sum", [P, 2, D])
        x_even = sb("x_even", [P, 2, D])
        x_odd = sb("x_odd", [P, 2, D])
        c_sum = sb("c_sum", [P, 2, D])
        c_even = sb("c_even", [P, 2, D])
        c_odd = sb("c_odd", [P, 2, D])
        x_f = sb("x_f", [P, NC, L])
        c_f = sb("c_f", [P, NC, L])
        kv_f = sb("kv_f", [P, NB, 4, 2 * D])
        prod = sb("prod", [P, 4, D])
        prod_sum = sb("prod_sum", [P, 2, 4, NB * H])
        cross = sb("cross", [P, 4, NB * H])
        corr_even = sb("corr_even", [GR, 2 * P])
        corr = sb("corr", [GR, L + 2])
        rest = sb("rest", [GR, L + 2])
        top = sb("top", [GR, 8])
        neg_top = sb("neg_top", [GR, 1])
        expd = sb("expd", [GR, L])
        chosen = sb("chosen", [GR, L])
        gsum = sb("gsum", [GR, 1])
        grec = sb("grec", [GR, 1])
        g_t = sb("g_t", [P, NA, NB * H])
        g_sum = sb("g_sum", [P, 2, NB * H])
        g_even = sb("g_even", [P, 2, NB * H])
        g_odd = sb("g_odd", [P, 2, NB * H])
        g_re = sb("g_re", [P, 2, NB * H])
        g_im = sb("g_im", [P, 2, NB * H])
        g_rx = sb("g_rx", [P, 2, NB * H])
        out_f = sb("out_f", [P, 2, 2, D])
        m_a = sb("m_a", [P, 2, D])
        m_b = sb("m_b", [P, 2, D])
        m_c = sb("m_c", [P, 2, D])
        m_d = sb("m_d", [P, 2, D])
        pm = sb("pm", [P, 2, 2 * P])
        out_t = sb("out_t", [P, NC, NA, P])
        var_all = sb("var_all", [P, NA])
        xc = sb("xc", [P, NA, D])
        wround = xc[:].rearrange("p a d -> p (a d)").bitcast(I16)
        xmax = sb("xmax", [P, NA])
        xr = sb("xr", [P, NA])
        xm = sb("xm", [P, NA])
        xscale = sb("xscale", [P, NA])
        xinv = sb("xinv", [P, NA])
        xv = sb("xv", [P, NA])
        xve = sb("xve", [P, NA])
        xraw = sb("xraw", [P, NA])
        xround = sb("xround", [P, NA, D], I16)
        xdeq = sb("xdeq", [P, NB, NA])
        xq = sb("xq", [P, NA, D], BF16)
        xq_t = sb("xq_t", [P, NB, NA, NC, P], BF16)
        hid = [w[:, k * FF:(k + 1) * FF] for w in (w1f, w2f) for k in range(2)]
        b1_part = sb("b1_part", [NPART, FF], BF16)
        b1_rows = sb("b1_rows", [NPART, FF], BF16)
        parts = sb("parts", [NPART, 2])
        aug = sb("aug", [P, NA, NPART], BF16)
        aug_t = sb("aug_t", [NPART, NB, NA, P], BF16)
        winv = sb("winv", [P, 1])
        s_part = sb("s_part", [P, NA])
        s_full = sb("s_full", [P, NA])
        hsquare = x_f[:].rearrange("p c n -> p (c n)")
        hss = sb("hss", [P, NA])
        hmax = sb("hmax", [P, NA])
        hr = sb("hr", [P, NA])
        hm = sb("hm", [P, NA])
        hms = sb("hms", [P, NA])
        hinv = sb("hinv", [P, NA])
        hscale = sb("hscale", [P, NA])
        hdeq = sb("hdeq", [P, NA])
        hround = c_f[:].rearrange("p c n -> p (c n)").bitcast(I16).rearrange("p (k n) -> p k n", k=2)
        hq = kv_f[:, 0, 0:2, :].rearrange("p t n -> p (t n)").bitcast(BF16).rearrange("p (k n) -> p k n", k=2)
        hq_t = kv_f[:, 0, 2:4, :].rearrange("p t n -> p (t n)").bitcast(BF16).rearrange("p (k c r) -> p k c r", k=2, c=NK)
        wsum = sb("wsum", [P, 2])
        wtot = sb("wtot", [P, 2])
        wmean = sb("wmean", [P, 2])
        wscale = sb("wscale", [P, 2])
        wdeq = sb("wdeq", [P, 2])
        half_neg = sb("half_neg", [P, NA])
        one_neg = sb("one_neg", [P, NA])
        eps = sb("eps", [P, 1])
        eps1 = sb("eps1", [P, NA])
        eps2 = sb("eps2", [P, NA])
        ones = sb("ones", [P, NA, 3])
        warm = sb("warm", [P, 1])
        zeros = sb("zeros", [P, L], BF16)

        psum = es.enter_context(nc.psum_tensor("psum", [P, 8, L], F32))

        def bank(i):
            return psum[:, i, :]
        K_BANKS, Q_BANKS, A_BANKS = 0, 4, 6
        I_BANKS, O_BANKS, X_BANKS = 6, 2, 4
        M_BANKS = (A_BANKS, 0)
        G_BANKS = (3, 1)
        H_BANKS, Y_BANKS, T_BANKS = 0, 4, 6

        def tile(m, j, back):
            return m - (back - j + NA - 1) // NA, (j - back) % NA, m * NA + (j - back)

        ROUNDED, TURNED, COPIED, SUMMED, FINISHED = 2, 3, 4, 5, 6

        def needed(count):
            return not isinstance(count, int) or count > 0

        def t_bank(i):
            return bank(T_BANKS + i).bitcast(BF16)

        def x_bank(i):
            return bank(X_BANKS + i).bitcast(BF16)

        def rows(g):
            return slice(g * GR, (g + 1) * GR)

        s = {}
        for name in ("c_fwd_in", "wq_in", "wkv_in", "bias_in", "late_in", "b1_in", "b1_step", "b1_made", "s_full_made", "s_hi_made", "s_part_made", "s_mid_made", "aug_made", "w1_in", "w2_in", "x_in0", "x_in1", "x_in2", "x_in3", "c_in0", "c_in1", "c_in2", "c_in3",
                     "consts", "zeros_made", "stats_made", "mv_made", "rstd_t", "rstd_made", "xn_made", "x_sum_made", "xs_made",
                     "c_sum_made", "cs_made", "spec_done", "spec_copied", "q_done", "kv_done", "kv_copied",
                     "bkv_made", "kv_biased", "q_biased", "prod_made", "prod_used", "res_made",
                     "wabs_made", "wtot_made", "wmean_made", "wdeq_made", "wscale_made", "w_step", "w_quantised",
                     "cross_made", "corr_done", "corr_even_copied", "corr_made", "max_made", "neg_made", "sent_made",
                     "rest_made", "exp_made", "mask_made", "gsum_made", "grec_made", "g_made", "g_t_done", "g_t_copied",
                     "g_sum_made", "gs_made", "g_f_done", "g_f_copied", "g_ready",
                     "m_ab", "out_re_made", "m_cd", "out_im_made", "at_done", "pm_copied", "at_used",
                     "stats2_made", "mv2_made", "xc_made", "xmax_made", "xv_made", "xve_made", "xr_made", "xraw_made", "xm_made", "xinv_made", "xscale_made", "xround", "xq_made", "b2_added",
                     "xt_done", "xt_copied", "h_done", "hid_made", "hss_made", "hmax_made", "hms_made", "hr_made", "hm_made", "hinv_made", "hdeq_made",
                     "hscale_made", "hround", "hq_made", "ht_done", "ht_copied", "y_done", "y_made",
                     "stored"):
            s[name] = sem(name)

        x_v = x.rearrange("b (a p) d -> p b a d", p=P)
        ctx_v = ctx.rearrange("b (a p) d -> p b a d", p=P)
        out_v = out.rearrange("b (a p) d -> p b a d", p=P)

        def by_heads(ap):
            return ap.rearrange("p f (h d) -> p f h d", d=DK)

        block = es.enter_context(nc.Block())

        @block.sync
        def _(sp):
            sp.dma_start(ctx_in[:, 0], ctx_v[:, 0]).then_inc(s["c_in0"], 16)
            sp.dma_start(forward[:], c_forward).then_inc(s["c_fwd_in"], 16)
            sp.dma_start(res[:, 0], x_v[:, 0]).then_inc(s["x_in0"], 16)
            sp.dma_start(wkv[:], wkv_t.rearrange("(c p) n -> p c n", p=P)).then_inc(s["wkv_in"], 16)
            sp.dma_start(wq[:], wq_t.rearrange("(c p) n -> p c n", p=P)).then_inc(s["wq_in"], 16)
            sp.dma_start(bq_row[:], bq.unsqueeze(0)).then_inc(s["bias_in"], 16)
            sp.dma_start(bkv_row[:], bkv.unsqueeze(0)).then_inc(s["bias_in"], 16)
            sp.dma_start(bo_all[:], bo.partition_broadcast(P)).then_inc(s["bias_in"], 16)
            sp.dma_start(b1_all[:], b1.partition_broadcast(NPART)).then_inc(s["b1_in"], 16)
            sp.dma_start(parts[:], c_parts).then_inc(s["b1_in"], 16)
            sp.dma_start(res[:, 1], x_v[:, 1]).then_inc(s["x_in1"], 16)
            sp.dma_start(ctx_in[:, 1], ctx_v[:, 1]).then_inc(s["c_in1"], 16)
            sp.dma_start(res[:, 2], x_v[:, 2]).then_inc(s["x_in2"], 16)
            sp.dma_start(w1f[:].rearrange("p (c n) -> p c n", c=NC), w1_t.rearrange("(c p) n -> p c n", p=P)).then_inc(s["w1_in"], 16)
            sp.dma_start(w2f[:].rearrange("p (c n) -> p c n", c=NK), w2_t.rearrange("(c p) n -> p c n", p=P)).then_inc(s["w2_in"], 16)
            sp.dma_start(res[:, 3], x_v[:, 3]).then_inc(s["x_in3"], 16)
            sp.dma_start(eye[:], c_eye).then_inc(s["late_in"], 16)
            sp.dma_start(to_signal[:], c_signal).then_inc(s["late_in"], 16)
            sp.dma_start(wo[:], wo_t.rearrange("(c p) n -> p c n", p=P)).then_inc(s["late_in"], 16)
            sp.dma_start(b2_all[:], b2.partition_broadcast(P)).then_inc(s["late_in"], 16)
            for n in (2, 3):
                sp.wait_ge(s["cs_made"], n - 1)
                sp.dma_start(ctx_in[:, n % 2], ctx_v[:, n]).then_inc(s[f"c_in{n}"], 16)
            with sp.Fori(0, NB) as m:
                for j in range(NA):
                    sp.wait_ge(s["y_made"], m * NA + (j + 1))
                    sp.dma_start(out_v[:, m, j], res[:, m, j]).then_inc(s["stored"], 16)
            sp.wait_ge(s["stored"], 16 * NA * NB)

        LATE = 4 * 16

        @block.tensor
        def _(pe):
            def spectrum(dst, even, odd, c, done):
                cols = slice(c * P, (c + 1) * P)
                parts = dst.rearrange("q (k f) -> q k f", k=4)
                pe.matmul(parts[:, 0:2, 0:64], even[:, 0, cols], forward[:, 0:128].rearrange("p (k f) -> p k f", k=2),
                          start=True, stop=False)
                pe.matmul(parts[:, 0:2, 64:128], even[:, 1, cols], forward[:, 128:256].rearrange("p (k f) -> p k f", k=2),
                          start=False, stop=False)
                pe.matmul(dst[:, 256:512], odd[:, 0, cols], forward[:, 256:512], start=False, stop=False)
                pe.matmul(dst[:, 256:512], odd[:, 1, cols], forward[:, 512:768], start=False, stop=True).then_inc(done, 1)

            def keep_busy(b, count):
                for _ in range(count):
                    pe.matmul(bank(b), zeros[:, 0:P], zeros[:], start=True, stop=True)

            pe.wait_ge(s["zeros_made"], 1)
            keep_busy(K_BANKS, 12)
            pe.wait_ge(s["c_fwd_in"], 16)
            def transform(n, before_kv=None, after_kv=None, after_q=None):
                for k in range(2):
                    even, odd, made = ((c_even, c_odd, s["cs_made"]), (x_even, x_odd, s["xs_made"]))[k]
                    pe.wait_ge(made, n + 1)
                    for c in range(NC):
                        if n or k:
                            pe.wait_ge(s["spec_copied"], n * 4 + (2 * k + c - 1))
                        if (n, k) == (3, 0):
                            pe.wait_ge(s["corr_made"], 1)
                        spectrum(bank(A_BANKS + c), even, odd, c, s["spec_done"])
                    if k == n == 0:
                        kv_spectra(0, 0)
                        kv_spectra(0, 1)
                if before_kv:
                    before_kv()
                if n:
                    kv_spectra(n, 0)
                if after_kv:
                    pe.wait_ge(s["spec_copied"], n * 4 + 4)
                    after_kv()
                q_spectra(n, 0)
                if after_q:
                    after_q()
                if n:
                    kv_spectra(n, 1)
                q_spectra(n, 1)

            def kv_spectra(n, fam):
                if fam == 0:
                    pe.wait_ge(s["wkv_in"], 16)
                    pe.wait_ge(s["spec_copied"], n * 4 + 2)
                for part in range(2):
                    ft = 2 * fam + part
                    if n:
                        pe.wait_ge(s["kv_copied"], n * 4 - 3 + ft)
                    for c in range(NC):
                        mm = pe.matmul(bank(K_BANKS + ft), c_f[:, c, ft * P:(ft + 1) * P], wkv[:, c, :],
                                       start=(c == 0), stop=(c == NC - 1))
                    mm.then_inc(s["kv_done"], 1)

            def q_spectra(n, fam):
                if fam == 0:
                    pe.wait_ge(s["wq_in"], 16)
                    pe.wait_ge(s["spec_copied"], n * 4 + 4)
                if n:
                    pe.wait_ge(s["prod_used"], n * 2 - 1 + fam)
                for part in range(2):
                    ft = 2 * fam + part
                    for c in range(NC):
                        mm = pe.matmul(psum[:, Q_BANKS + fam, part * D:(part + 1) * D], x_f[:, c, ft * P:(ft + 1) * P],
                                       wq[:, c, :], start=(c == 0), stop=(c == NC - 1))
                mm.then_inc(s["q_done"], 1)

            def correlate(g):
                pe.wait_ge(s["cross_made"], g * 4 + 4)
                pe.wait_ge(s["late_in"], LATE)
                if g:
                    pe.wait_ge(s["kv_copied"], 4 * NB)
                for fam in range(2):
                    for part in range(2):
                        ft = 2 * fam + part
                        mm = pe.matmul(psum[0:GR, M_BANKS[g] + 1 - fam, 0:2 * P], cross[:, ft, rows(g)], to_signal[:, ft, :],
                                       start=(part == 0), stop=(part == 1))
                    mm.then_inc(s["corr_done"], 1)

            def turn_g(g):
                pe.wait_ge(s["g_made"], g + 1)
                if g == 0:
                    pe.wait_ge(s["kv_copied"], 4 * (NB - 1))
                for a in range(NA):
                    mm = pe.transpose(psum[:, G_BANKS[g], a * GR:(a + 1) * GR], chosen[:, a * P:(a + 1) * P], eye[0:GR, 0:GR])
                mm.then_inc(s["g_t_done"], 1)

            def spectrum_g(g):
                pe.wait_ge(s["gs_made"], g * 2 + 2)
                gf = psum[:, M_BANKS[g], 0:4 * GR].rearrange("p (k n) -> p k n", k=4)
                r = rows(g)
                for part in range(2):
                    pe.matmul(gf[0:64, part, :], forward[:, part * 64:(part + 1) * 64], g_even[:, 0, r], start=True, stop=True)
                    pe.matmul(gf[64:128, part, :], forward[:, 128 + part * 64:128 + (part + 1) * 64], g_even[:, 1, r], start=True, stop=True)
                for part in range(2):
                    pe.matmul(gf[:, 2 + part, :], forward[:, 256 + part * P:256 + (part + 1) * P], g_odd[:, 0, r], start=True, stop=False)
                    mm = pe.matmul(gf[:, 2 + part, :], forward[:, 512 + part * P:512 + (part + 1) * P], g_odd[:, 1, r], start=False, stop=True)
                mm.then_inc(s["g_f_done"], 1)

            transform(0)
            transform(1)
            transform(2, after_q=lambda: correlate(0))
            transform(3, before_kv=lambda: turn_g(0), after_kv=lambda: spectrum_g(0))

            def inverse(n, c):
                if c == 0:
                    pe.wait_ge(s["out_re_made"], n + 1)
                    pe.wait_ge(s["out_im_made"], n + 1)
                if n:
                    pe.wait_ge(s["at_used"], n * 4 + (c - 3))
                else:
                    pe.wait_ge(s["g_f_copied"], 2)
                for ft in range(4):
                    fam, part = divmod(ft, 2)
                    mm = pe.matmul(psum[:, I_BANKS + c, fam * D:(fam + 1) * D], out_f[:, fam, part, c * P:(c + 1) * P],
                                   to_signal[:, ft, :], start=(ft == 0), stop=(ft == 3))
                mm.then_inc(s["at_done"], 1)

            def project(n, half):
                if half == 0:
                    pe.wait_ge(s["at_used"], n * 4 + 2)
                for k in range(2):
                    a = 2 * half + k
                    for c in range(NC):
                        mm = pe.matmul(psum[:, O_BANKS + half, k * D:(k + 1) * D], out_t[:, c, SLOT[a], :], wo[:, c, :],
                                       start=(c == 0), stop=(c == NC - 1))
                mm.then_inc(s["at_done"], 1)

            def turn_x(n):
                pe.wait_ge(s["aug_made"], n + 1)
                pe.wait_ge(s["xq_made"], n + 1)
                if n:
                    pe.wait_ge(s["xt_copied"], n * 2)
                t = x_bank(0).rearrange("p (a c r) -> p a c r", a=NA, c=NC)
                for a in range(NA):
                    for c in range(NC):
                        pe.transpose(t[:, a, c, :], xq[:, a, c * P:(c + 1) * P], eye16[:])
                for a in range(NA):
                    mm = pe.transpose(x_bank(1)[0:NPART, a * P:(a + 1) * P], aug[:, a, :], eye16[:])
                mm.then_inc(s["xt_done"], 1)

            inverse(0, 0)
            inverse(0, 1)
            correlate(1)
            project(0, 0)
            project(0, 1)
            inverse(1, 0)
            inverse(1, 1)
            turn_g(1)
            keep_busy(X_BANKS, 4)
            spectrum_g(1)
            project(1, 0)
            project(1, 1)
            pe.wait_ge(s["consts"], 3)
            for n in (2, 3):
                inverse(n, 0)
                inverse(n, 1)
                keep_busy(M_BANKS[1], 5)
                project(n, 0)
                project(n, 1)
                turn_x(n - 2)

            def up(m, j):
                _, _, t = tile(m, j, 0)
                if j == 0:
                    pe.wait_ge(s["xt_copied"], m * 2 + 2)
                if needed(t - 1):
                    pe.wait_ge(s["hid_made"], t - 1)
                for half in range(2):
                    cols = slice(half * L, (half + 1) * L)
                    dst = bank(H_BANKS + 2 * (j % 2) + half)
                    for c in range(NC):
                        pe.matmul(dst, xq_t[:, m, j, c, :], w1q[:, c, cols], start=(c == 0), stop=False)
                    mm = pe.matmul(dst, aug_t[:, m, j, :], b1_rows[:, cols], start=False, stop=True)
                mm.then_inc(s["h_done"], 1)

            def turn_h(m, j):
                m, j, t = tile(m, j, TURNED)
                pe.wait_ge(s["hq_made"], t + 1)
                if needed(t - 1):
                    pe.wait_ge(s["ht_copied"], t - 1)
                for k in range(NK):
                    mm = pe.transpose(t_bank(j % 2)[:, k * P:(k + 1) * P], hq[:, j % 2, k * P:(k + 1) * P], eye16[:])
                mm.then_inc(s["ht_done"], 1)

            def down(m, j):
                m, j, t = tile(m, j, SUMMED)
                pe.wait_ge(s["ht_copied"], t + 1)
                if needed(t - 1):
                    pe.wait_ge(s["y_made"], t - 1)
                for k in range(NK):
                    mm = pe.matmul(psum[:, Y_BANKS + j % 2, 0:D], hq_t[:, j % 2, k, :], w2q[:, k, :],
                                   start=(k == 0), stop=(k == NK - 1))
                mm.then_inc(s["y_done"], 1)

            pe.wait_ge(s["w_quantised"], 2)
            pe.wait_ge(s["b1_made"], 1)
            for m in (0, 1):
                for j in range(NA):
                    if (m, j) == (0, 1):
                        pe.wait_ge(s["at_used"], 4 * NB)
                    up(m, j)
                    if (m, j) == (0, 2):
                        keep_busy(T_BANKS + 1, 9)
                        turn_x(2)
                    if (m, j) == (1, 0):
                        pe.wait_ge(s["xt_copied"], 6)
                        keep_busy(X_BANKS, 10)
                        turn_x(3)
                    if (m, j) == (1, 1):
                        pe.wait_ge(s["xt_copied"], 2 * NB)
                    if NA * m + j >= SUMMED:
                        down(m, j)
                    if NA * m + j >= TURNED:
                        turn_h(m, j)
            with pe.Fori(2, NB) as m:
                for j in range(NA):
                    up(m, j)
                    down(m, j)
                    turn_h(m, j)
            for j in range(SUMMED):
                down(NB, j)
                if j < TURNED:
                    turn_h(NB, j)

        @block.scalar
        def _(act):
            def copy_spectra(n, k):
                for c in range(NC):
                    act.wait_ge(s["spec_done"], n * 4 + (2 * k + c + 1))
                    act.copy((c_f, x_f)[k][:, c, :], bank(A_BANKS + c)).then_inc(s["spec_copied"], 1)

            def copy_kv(n, ft):
                act.wait_ge(s["kv_done"], n * 4 + (ft + 1))
                act.copy(kv_f[:, n, ft, :], bank(K_BANKS + ft)).then_inc(s["kv_copied"], 1)

            def exponents(g):
                act.wait_ge(s["neg_made"], g + 1)
                act.wait_ge(s["corr_made"], g + 1)
                act.activation(expd[:], corr[:, 0:L], ACT.Exp, bias=neg_top[:, 0:1], scale=1.0 / DK).then_inc(s["exp_made"], 1)

            def copy_corr_even(g):
                act.wait_ge(s["corr_done"], g * 2 + 1)
                act.copy(corr_even[:], psum[0:GR, M_BANKS[g] + 1, 0:2 * P]).then_inc(s["corr_even_copied"], 1)

            def copy_g(g):
                act.wait_ge(s["g_t_done"], g + 1)
                act.copy(g_t[:, :, rows(g)], psum[:, G_BANKS[g], 0:NA * GR].rearrange("p (a n) -> p a n", a=NA)).then_inc(s["g_t_copied"], 1)

            act.wait_ge(s["consts"], 1)
            act.activation(warm[:], half_neg[:, 0:1], ACT.Exp)
            for n in range(NB):
                copy_spectra(n, 0)
                if n:
                    copy_spectra(n, 1)
                if n == 3:
                    copy_g(0)
                for ft in range(4):
                    if (n, ft) == (2, 2):
                        copy_corr_even(0)
                    copy_kv(n, ft)
                if n == 0:
                    copy_spectra(n, 1)
                if n == 2:
                    exponents(0)

            def inverse_copy(n, c):
                act.wait_ge(s["at_done"], n * 4 + (c + 1))
                act.copy(pm[:, c], psum[:, I_BANKS + c, 0:2 * P]).then_inc(s["pm_copied"], 1)

            def centre(n):
                act.wait_ge(s["mv2_made"], n + 1)
                if n:
                    act.wait_ge(s["xround"], n)
                for a in range(NA):
                    ins = act.activation(xc[:, a, :], res[:, n, a, :], ACT.Identity, bias=mv[:, a, 0:1], scale=-1.0)
                ins.then_inc(s["xc_made"], 1)

            def copy_x(n):
                act.wait_ge(s["xt_done"], n + 1)
                act.copy(aug_t[:, n].rearrange("k a r -> k (a r)").bitcast(I32), x_bank(1)[0:NPART, 0:NA * P].bitcast(I32)).then_inc(s["xt_copied"], 1)
                act.copy(xq_t[:, n].rearrange("p a c r -> p (a c r)").bitcast(I32), x_bank(0).bitcast(I32)).then_inc(s["xt_copied"], 1)

            inverse_copy(0, 0)
            inverse_copy(0, 1)
            copy_corr_even(1)
            exponents(1)
            act.activation(warm[:], half_neg[:, 0:1], ACT.Gelu)
            inverse_copy(1, 0)
            inverse_copy(1, 1)
            copy_g(1)
            centre(0)
            inverse_copy(2, 0)
            inverse_copy(2, 1)
            centre(1)
            copy_x(0)
            inverse_copy(3, 0)
            inverse_copy(3, 1)
            centre(2)
            copy_x(1)
            def gelu(m, j):
                _, _, t = tile(m, j, 0)
                act.wait_ge(s["h_done"], t + 1)
                if needed(t - 3):
                    act.wait_ge(s["hq_made"], t - 3)
                hb = psum[:, H_BANKS + 2 * (j % 2):H_BANKS + 2 * (j % 2) + 2, :].rearrange("p k n -> p (k n)")
                act.activation(hid[j], hb, ACT.Gelu, scale=xdeq[:, m, j:j + 1]).then_inc(s["hid_made"], 1)

            def square(m, j):
                _, _, t = tile(m, j, 0)
                act.wait_ge(s["hid_made"], t + 1)
                act.activation(hsquare, hid[j], ACT.Square, scale=FF ** -0.5, accum_out=hss[:, j:j + 1]).then_inc(s["hss_made"], 1)

            def copy_h(m, j):
                m, j, t = tile(m, j, COPIED)
                act.wait_ge(s["ht_done"], t + 1)
                if needed(t - 1):
                    act.wait_ge(s["y_done"], t - 1)
                act.copy(hq_t[:, j % 2].rearrange("p k r -> p (k r)").bitcast(I32), t_bank(j % 2).bitcast(I32)).then_inc(s["ht_copied"], 1)

            for m in (0, 1):
                for j in range(NA):
                    gelu(m, j)
                    if NA * m + j >= COPIED:
                        copy_h(m, j)
                    if (m, j) == (1, 0):
                        copy_x(3)
                    if (m, j) == (0, 2):
                        centre(3)
                    square(m, j)
                    if (m, j) == (0, 2):
                        copy_x(2)
            with act.Fori(2, NB) as m:
                for j in range(NA):
                    gelu(m, j)
                    copy_h(m, j)
                    square(m, j)
            for j in range(COPIED):
                copy_h(NB, j)

        @block.vector
        def _(dve):
            def normalise(n, between=None):
                for a in range(NA):
                    ins = dve.bn_stats(stats[:, a, :], res[:, n, a, :])
                ins.then_inc(s["stats_made"], 1)
                dve.wait_ge(s["stats_made"], n + 1)
                for a in range(NA):
                    ins = dve.bn_aggr(mv[:, a, :], stats[:, a, :])
                ins.then_inc(s["mv_made"], 1)
                if between:
                    between()
                dve.wait_ge(s["rstd_made"], n + 1)
                for a in range(NA):
                    ins = dve.tensor_scalar(xn[:, a, :], res[:, n, a, :], mv[:, a, 0:1], rstd[:, a:a + 1], ALU.subtract, ALU.mult)
                ins.then_inc(s["xn_made"], 1)

            def combine_x(n):
                dve.wait_ge(s["xn_made"], n + 1)
                dve.tensor_tensor(x_sum[:], xn[:, 0:2, :], xn[:, 2:4, :], ALU.add).then_inc(s["x_sum_made"], 1)
                if n:
                    dve.wait_ge(s["spec_done"], n * 4)
                dve.tensor_tensor(x_odd[:], xn[:, 0:2, :], xn[:, 2:4, :], ALU.subtract)
                dve.wait_ge(s["x_sum_made"], n + 1)
                dve.tensor_tensor(x_even[:, 0, :], x_sum[:, 0, :], x_sum[:, 1, :], ALU.add)
                dve.tensor_tensor(x_even[:, 1, :], x_sum[:, 0, :], x_sum[:, 1, :], ALU.subtract).then_inc(s["xs_made"], 1)

            def multiply(n):
                for fam in range(2):
                    q = psum[:, Q_BANKS + fam, :].rearrange("p (k d) -> p k d", k=2)
                    k_re, k_im = kv_f[:, n, 2 * fam, 0:D], kv_f[:, n, 2 * fam + 1, 0:D]
                    dve.wait_ge(s["q_done"], n * 2 + (fam + 1))
                    if fam == 0:
                        dve.scalar_tensor_tensor(q[0:1, 0, :], bq_row[:], float(L), q[0:1, 0, :], ALU.mult, ALU.add).then_inc(s["q_biased"], 1)
                        dve.wait_ge(s["kv_biased"], n + 1)
                        dve.wait_ge(s["q_biased"], n + 1)
                    dve.wait_ge(s["kv_copied"], n * 4 + (2 * fam + 2))
                    dve.tensor_tensor(prod[:, 0:2, :], q, kv_f[:, n, 2 * fam:2 * fam + 2, 0:D], ALU.mult)
                    dve.tensor_tensor(prod[:, 2, :], q[:, 1, :], k_re, ALU.mult)
                    dve.tensor_tensor(prod[:, 3, :], q[:, 0, :], k_im, ALU.mult).then_inc(s["prod_made"], 1)
                    dve.wait_ge(s["prod_made"], n * 2 + (fam + 1))
                    dve.tensor_reduce(prod_sum[:, fam, :, bass.ds(n * H, H)], prod[:].rearrange("p k (h d) -> p k h d", d=DK),
                                      AX.X, ALU.add).then_inc(s["prod_used"], 1)
                    dve.wait_ge(s["prod_used"], n * 2 + (fam + 1))

            dve.memset(zeros[:], 0.0).then_inc(s["zeros_made"], 1)
            dve.memset(half_neg[:], -0.5)
            dve.memset(eps[:], EPS)
            dve.memset(eps1[:], 1.0 + EPS)
            dve.memset(eps2[:], EPS * EPS)
            dve.memset(ones[:], 1.0)
            dve.memset(one_neg[:], -1.0).then_inc(s["consts"], 1)
            dve.memset(corr[:, L:L + 2], ABSENT).then_inc(s["consts"], 1)
            def sum_weights():
                for k, (w, arrived) in enumerate(((w1f, s["w1_in"]), (w2f, s["w2_in"]))):
                    dve.wait_ge(arrived, 16)
                    dve.tensor_reduce(wsum[:, k:k + 1], w[:], AX.X, ALU.add, apply_absolute_value=True).then_inc(s["wabs_made"], 1)

            def quantise_weights():
                dve.wait_ge(s["wtot_made"], 1)
                dve.tensor_scalar(wmean[:], wtot[:], 1.0 / (D * FF), 1e-5, ALU.mult, ALU.max).then_inc(s["wmean_made"], 1)
                dve.wait_ge(s["wmean_made"], 1)
                dve.tensor_scalar(wdeq[:], wmean[:], 1.0 / 127.0, None, ALU.mult).then_inc(s["wdeq_made"], 1)
                dve.wait_ge(s["wdeq_made"], 1)
                dve.reciprocal(winv[:], wdeq[:, 0:1])
                dve.reciprocal(wscale[:], wmean[:]).then_inc(s["wscale_made"], 1)
                dve.wait_ge(s["wscale_made"], 1)
                for k, (w, wq_) in enumerate(((w1f, w1q), (w2f, w2q))):
                    dve.tensor_scalar(wround, w[:], wscale[:, k:k + 1], 1.0, ALU.mult, ALU.min).then_inc(s["w_step"], 1)
                    dve.wait_ge(s["w_step"], k + 1)
                    dve.tensor_scalar(wq_[:].rearrange("p c n -> p (c n)"), wround, -1.0, None, ALU.max).then_inc(s["w_quantised"], 1)
                    dve.wait_ge(s["w_quantised"], k + 1)

            def part_b1():
                dve.wait_ge(s["b1_in"], 32)
                dve.tensor_copy(b1_part[:], b1_all[:]).then_inc(s["b1_step"], 1)
                dve.wait_ge(s["b1_step"], 1)
                dve.scalar_tensor_tensor(b1_all[:], b1_part[:], parts[:, 0:1], b1_all[:], ALU.mult, ALU.add).then_inc(s["b1_step"], 1)

            def part_b1_again():
                dve.wait_ge(s["b1_step"], 2)
                dve.tensor_copy(b1_part[:], b1_all[:]).then_inc(s["b1_step"], 1)
                dve.wait_ge(s["b1_step"], 3)
                dve.scalar_tensor_tensor(b1_rows[:], b1_part[:], parts[:, 1:2], b1_all[:], ALU.mult, ALU.add).then_inc(s["b1_made"], 1)

            def cross_spectra(g):
                r = rows(g)
                e_re, e_im = cross[:, RE_E:RE_O + 1:2, r], cross[:, IM_E:IM_O + 1:2, r]
                dve.tensor_tensor(e_re, prod_sum[:, :, 0, r], prod_sum[:, :, 1, r], ALU.add).then_inc(s["cross_made"], 1)
                dve.tensor_tensor(e_im, prod_sum[:, :, 2, r], prod_sum[:, :, 3, r], ALU.subtract).then_inc(s["cross_made"], 1)
                dve.wait_ge(s["cross_made"], g * 4 + 2)
                dve.tensor_copy(cross[0:1, RE_E, r], prod_sum[0:1, 0, 0, r]).then_inc(s["cross_made"], 1)
                dve.tensor_copy(cross[0:1, IM_E, r], prod_sum[0:1, 0, 1, r]).then_inc(s["cross_made"], 1)

            def choose(g):
                dve.wait_ge(s["corr_even_copied"], g + 1)
                dve.wait_ge(s["corr_done"], g * 2 + 2)
                even = corr_even[:].rearrange("n (a t) -> n a t", a=2)
                odd = psum[0:GR, M_BANKS[g], 0:2 * P].rearrange("n (a t) -> n a t", a=2)
                delays = corr[:, 0:L].rearrange("n (a t) -> n a t", a=NA)
                dve.tensor_tensor(delays[:, 0:4:3], even, odd, ALU.add)
                dve.tensor_tensor(delays[:, 2], even[:, 0], odd[:, 0], ALU.subtract)
                dve.tensor_tensor(delays[:, 1], even[:, 1], odd[:, 1], ALU.subtract).then_inc(s["corr_made"], 1)
                dve.wait_ge(s["corr_made"], g + 1)
                dve.max(top[:], corr[:, 0:L]).then_inc(s["max_made"], 1)
                dve.wait_ge(s["max_made"], g + 1)
                dve.tensor_scalar(neg_top[:], top[:, 0:1], -1.0 / DK, None, ALU.mult).then_inc(s["neg_made"], 1)
                dve.memset(top[:, TOPK:8], ABSENT).then_inc(s["sent_made"], 1)
                dve.wait_ge(s["sent_made"], g + 1)
                dve.match_replace(rest[:], top[:], corr[:], -1.0e38).then_inc(s["rest_made"], 1)
                dve.wait_ge(s["rest_made"], g + 1)
                dve.tensor_tensor(rest[:, 0:L], corr[:, 0:L], rest[:, 0:L], ALU.not_equal).then_inc(s["mask_made"], 1)

            def weigh(g):
                dve.wait_ge(s["mask_made"], g + 1)
                dve.wait_ge(s["exp_made"], g + 1)
                dve.tensor_tensor_reduce(out=expd[:], in0=expd[:], in1=rest[:, 0:L], scale=1.0, scalar=0.0,
                                         op0=ALU.mult, op1=ALU.add, accum_out=gsum[:]).then_inc(s["gsum_made"], 1)
                dve.wait_ge(s["gsum_made"], g + 1)
                dve.reciprocal(grec[:], gsum[:]).then_inc(s["grec_made"], 1)
                dve.wait_ge(s["grec_made"], g + 1)
                dve.tensor_scalar(chosen[:], expd[:], grec[:, 0:1], None, ALU.mult).then_inc(s["g_made"], 1)

            def combine_g(g):
                r = rows(g)
                dve.wait_ge(s["g_t_copied"], g + 1)
                dve.tensor_tensor(g_sum[:, :, r], g_t[:, 0:2, r], g_t[:, 2:4, r], ALU.add).then_inc(s["g_sum_made"], 1)
                dve.tensor_tensor(g_odd[:, :, r], g_t[:, 0:2, r], g_t[:, 2:4, r], ALU.subtract).then_inc(s["gs_made"], 1)
                dve.wait_ge(s["g_sum_made"], g + 1)
                dve.tensor_tensor(g_even[:, 0, r], g_sum[:, 0, r], g_sum[:, 1, r], ALU.add)
                dve.tensor_tensor(g_even[:, 1, r], g_sum[:, 0, r], g_sum[:, 1, r], ALU.subtract).then_inc(s["gs_made"], 1)

            def copy_g_spectrum(g):
                r = rows(g)
                dve.wait_ge(s["g_f_done"], g + 1)
                gf = psum[:, M_BANKS[g], 0:4 * GR].rearrange("p (f k n) -> p f k n", f=2, k=2)
                dve.tensor_copy(g_re[:, :, r], gf[:, :, 0, :]).then_inc(s["g_f_copied"], 1)
                dve.tensor_copy(g_im[:, :, r], gf[:, :, 1, :]).then_inc(s["g_f_copied"], 1)
                dve.wait_ge(s["g_f_copied"], g * 2 + 2)
                dve.tensor_copy(g_rx[:, :, r], g_re[:, :, r]).then_inc(s["g_ready"], 1)
                dve.wait_ge(s["g_ready"], g * 3 + 1)
                dve.tensor_copy(g_rx[0:1, 0, r], g_im[0:1, 0, r]).then_inc(s["g_ready"], 1)
                dve.wait_ge(s["g_ready"], g * 3 + 2)
                dve.memset(g_im[0:1, 0, r], 0.0).then_inc(s["g_ready"], 1)

            def g_of(g, n):
                return g[:, :, bass.ds(n * H, H)].unsqueeze(3).broadcast_to([P, 2, H, DK])

            def v_of(n, part):
                return by_heads(kv_f[:, n, part:part + 3:2, D:2 * D])

            def out_re_products(n):
                if n % (NB // NG) == 0:
                    dve.wait_ge(s["g_ready"], n // (NB // NG) * 3 + 3)
                if n:
                    dve.wait_ge(s["out_re_made"], n)
                dve.tensor_tensor(by_heads(m_a[:]), v_of(n, 0), g_of(g_re, n), ALU.mult)
                dve.tensor_tensor(by_heads(m_b[:]), v_of(n, 1), g_of(g_im, n), ALU.mult).then_inc(s["m_ab"], 1)

            def out_re(n):
                dve.wait_ge(s["m_ab"], n + 1)
                if n:
                    dve.wait_ge(s["at_done"], n * 4 - 2)
                dve.tensor_tensor(out_f[:, :, 0, :], m_a[:], m_b[:], ALU.subtract).then_inc(s["out_re_made"], 1)

            def inverse_out(n, c):
                dve.wait_ge(s["pm_copied"], n * 2 + (c + 1))
                odd = psum[:, I_BANKS + c, 2 * P:4 * P]
                dve.tensor_tensor(out_t[:, c, 0:2].rearrange("p a t -> p (a t)"), pm[:, c], odd, ALU.add)
                dve.tensor_tensor(out_t[:, c, 2:4].rearrange("p a t -> p (a t)"), pm[:, c], odd, ALU.subtract).then_inc(s["at_used"], 1)

            def add_residual(n, half):
                dve.wait_ge(s["at_done"], n * 4 + (3 + half))
                if half == 0:
                    dve.wait_ge(s["res_made"], n + 1)
                x1 = res[:, n, 2 * half:2 * half + 2, :].rearrange("p a d -> p (a d)")
                dve.tensor_tensor(x1, x1, bank(O_BANKS + half), ALU.add).then_inc(s["at_used"], 1)

            def stats2(n):
                dve.wait_ge(s["at_used"], n * 4 + 4)
                for a in range(NA):
                    ins = dve.bn_stats(stats[:, a, :], res[:, n, a, :])
                ins.then_inc(s["stats2_made"], 1)

            def mean_var2(n):
                dve.wait_ge(s["stats2_made"], n + 1)
                if n:
                    dve.wait_ge(s["xv_made"], n)
                for a in range(NA):
                    ins = dve.bn_aggr(mv[:, a, :], stats[:, a, :])
                ins.then_inc(s["mv2_made"], 1)

            def row_max(n):
                dve.wait_ge(s["xc_made"], n + 1)
                dve.tensor_reduce(xmax[:], xc[:], AX.X, ALU.max, apply_absolute_value=True).then_inc(s["xmax_made"], 1)

            def x_raw(n):
                dve.wait_ge(s["xmax_made"], n + 1)
                dve.wait_ge(s["xr_made"], n + 1)
                dve.tensor_tensor(xraw[:], xmax[:], xr[:], ALU.mult).then_inc(s["xraw_made"], 1)

            def x_clip(n):
                dve.wait_ge(s["xraw_made"], n + 1)
                dve.tensor_scalar(xm[:], xraw[:], 1e-5, None, ALU.max).then_inc(s["xm_made"], 1)

            def x_inverse(n):
                dve.wait_ge(s["xm_made"], n + 1)
                if n:
                    dve.wait_ge(s["s_full_made"], n)
                dve.reciprocal(xinv[:], xm[:]).then_inc(s["xinv_made"], 1)
                dve.tensor_scalar(xdeq[:, n], xm[:], wdeq[:, 0:1], None, ALU.mult)

            def x_scale(n):
                dve.wait_ge(s["xinv_made"], n + 1)
                dve.scalar_tensor_tensor(xscale[:], xinv[:], -127.0, xr[:], ALU.mult, ALU.mult).then_inc(s["xscale_made"], 1)

            def quantise_x(n):
                dve.wait_ge(s["xscale_made"], n + 1)
                if n:
                    dve.wait_ge(s["xq_made"], n)
                for a in range(NA):
                    ins = dve.tensor_scalar(xround[:, a, :], xc[:, a, :], xscale[:, a:a + 1], None, ALU.mult)
                ins.then_inc(s["xround"], 1)
                dve.wait_ge(s["xround"], n + 1)
                if n:
                    dve.wait_ge(s["xt_done"], n)
                dve.tensor_copy(xq[:].rearrange("p a d -> p (a d)"), xround[:].rearrange("p a d -> p (a d)")).then_inc(s["xq_made"], 1)

            dve.wait_ge(s["c_in0"], 16)
            dve.tensor_tensor(c_sum[:], ctx_in[:, 0, 0:2, :], ctx_in[:, 0, 2:4, :], ALU.add).then_inc(s["c_sum_made"], 1)
            dve.tensor_tensor(c_odd[:], ctx_in[:, 0, 0:2, :], ctx_in[:, 0, 2:4, :], ALU.subtract)
            dve.wait_ge(s["c_sum_made"], 1)
            dve.tensor_tensor(c_even[:, 0, :], c_sum[:, 0, :], c_sum[:, 1, :], ALU.add)
            dve.tensor_tensor(c_even[:, 1, :], c_sum[:, 0, :], c_sum[:, 1, :], ALU.subtract).then_inc(s["cs_made"], 1)
            dve.wait_ge(s["x_in0"], 16)
            normalise(0)
            combine_x(0)
            dve.wait_ge(s["bias_in"], 48)
            dve.tensor_scalar(bkv_dc[:], bkv_row[:], float(L), None, ALU.mult).then_inc(s["bkv_made"], 1)
            dve.wait_ge(s["x_in1"], 16)
            normalise(1, between=part_b1)
            combine_x(1)
            sum_weights()
            multiply(0)
            dve.wait_ge(s["x_in2"], 16)
            normalise(2, between=part_b1_again)
            combine_x(2)
            quantise_weights()
            multiply(1)
            cross_spectra(0)
            dve.wait_ge(s["x_in3"], 16)
            normalise(3, between=lambda: choose(0))
            combine_x(3)
            weigh(0)
            dve.wait_ge(s["late_in"], LATE)
            dve.tensor_copy(eye16[:], eye[:]).then_inc(s["consts"], 1)
            multiply(2)
            combine_g(0)
            copy_g_spectrum(0)
            out_re_products(0)
            out_re(0)
            multiply(3)
            cross_spectra(1)

            inverse_out(0, 0)
            inverse_out(0, 1)
            out_re_products(1)
            out_re(1)
            choose(1)
            weigh(1)
            add_residual(0, 0)
            add_residual(0, 1)
            combine_g(1)
            inverse_out(1, 0)
            inverse_out(1, 1)
            copy_g_spectrum(1)
            out_re_products(2)
            out_re(2)
            stats2(0)
            mean_var2(0)
            for n in (2, 3):
                add_residual(n - 1, 0)
                add_residual(n - 1, 1)
                stats2(n - 1)
                row_max(n - 2)
                inverse_out(n, 0)
                x_raw(n - 2)
                inverse_out(n, 1)
                if n + 1 < NB:
                    out_re_products(n + 1)
                x_clip(n - 2)
                if n + 1 < NB:
                    out_re(n + 1)
                x_inverse(n - 2)
                x_scale(n - 2)
                quantise_x(n - 2)
                mean_var2(n - 1)
            add_residual(3, 0)
            add_residual(3, 1)
            stats2(3)
            row_max(2)
            x_raw(2)
            x_clip(2)
            x_inverse(2)
            x_scale(2)

            def hidden_max(m, j):
                _, _, t = tile(m, j, 0)
                dve.wait_ge(s["hid_made"], t + 1)
                dve.tensor_reduce(hmax[:, j:j + 1], hid[j], AX.X, ALU.max, apply_absolute_value=True).then_inc(s["hmax_made"], 1)

            def quantise_h(m, j):
                m, j, t = tile(m, j, ROUNDED)
                dve.wait_ge(s["hscale_made"], t + 1)
                dve.tensor_scalar(hround[:, j % 2, :], hid[j], hscale[:, j:j + 1], 127.0, ALU.mult, ALU.mult).then_inc(s["hround"], 1)

            def whole_h(m, j):
                m, j, t = tile(m, j, ROUNDED)
                dve.wait_ge(s["hround"], t + 1)
                if needed(t - 1):
                    dve.wait_ge(s["ht_done"], t - 1)
                dve.tensor_copy(hq[:, j % 2, :], hround[:, j % 2, :]).then_inc(s["hq_made"], 1)

            def finish(m, j):
                m, j, t = tile(m, j, FINISHED)
                dve.wait_ge(s["y_done"], t + 1)
                dve.wait_ge(s["hdeq_made"], t + 1)
                dve.wait_ge(s["b2_added"], t + 1)
                dve.scalar_tensor_tensor(res[:, m, j, :], psum[:, Y_BANKS + j % 2, 0:D], hdeq[:, j:j + 1],
                                         res[:, m, j, :], ALU.mult, ALU.add).then_inc(s["y_made"], 1)

            hidden_max(0, 0)
            quantise_x(2)
            mean_var2(3)
            hidden_max(0, 1)
            quantise_h(0, 2)
            whole_h(0, 2)
            row_max(3)
            x_raw(3)
            hidden_max(0, 2)
            x_clip(3)
            x_inverse(3)
            x_scale(3)
            quantise_x(3)
            quantise_h(0, 3)
            whole_h(0, 3)
            hidden_max(0, 3)
            for j in range(NA):
                if NA + j >= FINISHED:
                    finish(1, j)
                quantise_h(1, j)
                hidden_max(1, j)
                whole_h(1, j)
            with dve.Fori(2, NB) as m:
                for j in range(NA):
                    finish(m, j)
                    quantise_h(m, j)
                    hidden_max(m, j)
                    whole_h(m, j)
            for j in range(FINISHED):
                finish(NB, j)
                if j < ROUNDED:
                    quantise_h(NB, j)
                    whole_h(NB, j)

        @block.gpsimd
        def _(pool):
            def layer_rstd(n):
                pool.wait_ge(s["mv_made"], n + 1)
                pool.tensor_scalar(var_all[:], mv[:, :, 1], 1.0, EPS, ALU.mult, ALU.add).then_inc(s["rstd_t"], 1)
                pool.wait_ge(s["rstd_t"], n + 1)
                pool.tensor_tensor(rstd[:], var_all[:], half_neg[:], ALU.pow).then_inc(s["rstd_made"], 1)

            def combine(n):
                p = n % 2
                pool.wait_ge(s[f"c_in{n}"], 16)
                pool.wait_ge(s["cs_made"], n)
                pool.tensor_tensor(c_sum[:], ctx_in[:, p, 0:2, :], ctx_in[:, p, 2:4, :], ALU.add).then_inc(s["c_sum_made"], 1)
                if n:
                    pool.wait_ge(s["spec_done"], n * 4 - 2)
                pool.tensor_tensor(c_odd[:], ctx_in[:, p, 0:2, :], ctx_in[:, p, 2:4, :], ALU.subtract)
                pool.wait_ge(s["c_sum_made"], n + 1)
                pool.tensor_tensor(c_even[:, 0, :], c_sum[:, 0, :], c_sum[:, 1, :], ALU.add)
                pool.tensor_tensor(c_even[:, 1, :], c_sum[:, 0, :], c_sum[:, 1, :], ALU.subtract).then_inc(s["cs_made"], 1)

            def bias_kv(n):
                pool.wait_ge(s["kv_copied"], n * 4 + 1)
                row = kv_f[0:1, n, RE_E, :]
                pool.tensor_tensor(row, row, bkv_dc[:], ALU.add).then_inc(s["kv_biased"], 1)

            def bias_res(n):
                pool.wait_ge(s["xn_made"], n + 1)
                pool.tensor_tensor(res[:, n], res[:, n], bo_all[:].unsqueeze(1).broadcast_to([P, NA, D]), ALU.add).then_inc(s["res_made"], 1)

            pool.wait_ge(s["consts"], 1)
            layer_rstd(0)
            for n in range(NB):
                if n == 2:
                    combine(3)
                if n + 1 < NB:
                    layer_rstd(n + 1)
                if n == 0:
                    pool.wait_ge(s["bkv_made"], 1)
                bias_kv(n)
                if n < 2:
                    combine(n + 1)
                if n == 0:
                    pool.wait_ge(s["wabs_made"], 2)
                    pool.partition_all_reduce(wtot[:], wsum[:], P, bass.bass_isa.ReduceOp.add).then_inc(s["wtot_made"], 1)
                bias_res(n)

            def g_of(g, n):
                return g[:, :, bass.ds(n * H, H)].unsqueeze(3).broadcast_to([P, 2, H, DK])

            def v_of(n, part):
                return by_heads(kv_f[:, n, part:part + 3:2, D:2 * D])

            def out_im_products(n):
                if n % (NB // NG) == 0:
                    pool.wait_ge(s["g_ready"], n // (NB // NG) * 3 + 3)
                if n:
                    pool.wait_ge(s["out_im_made"], n)
                pool.tensor_tensor(by_heads(m_c[:]), v_of(n, 1), g_of(g_rx, n), ALU.mult)
                pool.tensor_tensor(by_heads(m_d[:]), v_of(n, 0), g_of(g_im, n), ALU.mult).then_inc(s["m_cd"], 1)

            def out_im(n):
                pool.wait_ge(s["m_cd"], n + 1)
                if n:
                    pool.wait_ge(s["at_done"], n * 4 - 2)
                pool.tensor_tensor(out_f[:, :, 1, :], m_c[:], m_d[:], ALU.add).then_inc(s["out_im_made"], 1)

            def h_math(m, j, others=False):
                p = slice(j, j + 1)
                _, _, t = tile(m, j, 0)
                pool.wait_ge(s["hss_made"], t + 1)
                pool.tensor_tensor(hms[:, p], hss[:, p], eps[:, 0:1], ALU.add).then_inc(s["hms_made"], 1)
                if others:
                    h_deq(m, j)
                pool.wait_ge(s["hms_made"], t + 1)
                pool.tensor_tensor(hr[:, p], hms[:, p], half_neg[:, 0:1], ALU.pow).then_inc(s["hr_made"], 1)
                pool.wait_ge(s["hmax_made"], t + 1)
                pool.wait_ge(s["hr_made"], t + 1)
                if others:
                    add_b2(m, j)
                pool.tensor_scalar(hm[:, p], hmax[:, p], hr[:, p], 1e-5, ALU.mult, ALU.max).then_inc(s["hm_made"], 1)
                pool.wait_ge(s["hm_made"], t + 1)
                pool.tensor_tensor(hinv[:, p], hm[:, p], one_neg[:, 0:1], ALU.pow).then_inc(s["hinv_made"], 1)
                pool.wait_ge(s["hinv_made"], t + 1)
                pool.tensor_tensor(hscale[:, p], hinv[:, p], hr[:, p], ALU.mult).then_inc(s["hscale_made"], 1)

            def h_deq(m, j):
                m, j, t = tile(m, j, TURNED)
                if needed(t - 3):
                    pool.wait_ge(s["y_made"], t - 3)
                p = slice(j, j + 1)
                pool.tensor_tensor(hdeq[:, p], hm[:, p], wdeq[:, 1:2], ALU.mult).then_inc(s["hdeq_made"], 1)

            def x_rms(n):
                pool.wait_ge(s["mv2_made"], n + 1)
                pool.tensor_tensor(xv[:], mv[:, :, 1], eps1[:], ALU.mult).then_inc(s["xv_made"], 1)
                pool.wait_ge(s["xv_made"], n + 1)
                pool.tensor_tensor(xve[:], xv[:], eps2[:], ALU.add).then_inc(s["xve_made"], 1)
                pool.wait_ge(s["xve_made"], n + 1)
                if n:
                    pool.wait_ge(s["xscale_made"], n)
                pool.tensor_tensor(xr[:], xve[:], half_neg[:], ALU.pow).then_inc(s["xr_made"], 1)

            def aug_parts(n):
                pool.wait_ge(s["xinv_made"], n + 1)
                pool.tensor_tensor(s_full[:], xinv[:], winv[:].broadcast_to([P, NA]), ALU.mult).then_inc(s["s_full_made"], 1)
                if n:
                    pool.wait_ge(s["xt_done"], n)
                pool.wait_ge(s["s_full_made"], n + 1)
                pool.tensor_tensor(aug[:, :, 0:3], s_full[:].unsqueeze(2).broadcast_to([P, NA, 3]), ones[:], ALU.mult).then_inc(s["s_hi_made"], 1)
                pool.wait_ge(s["s_hi_made"], n + 1)
                pool.tensor_tensor(s_part[:], s_full[:], aug[:, :, 0], ALU.subtract).then_inc(s["s_part_made"], 1)
                pool.wait_ge(s["s_part_made"], n + 1)
                pool.tensor_tensor(aug[:, :, 3:5], s_part[:].unsqueeze(2).broadcast_to([P, NA, 2]), ones[:, :, 0:2], ALU.mult).then_inc(s["s_mid_made"], 1)
                pool.wait_ge(s["s_mid_made"], n + 1)
                pool.tensor_tensor(aug[:, :, 5], s_part[:], aug[:, :, 3], ALU.subtract).then_inc(s["aug_made"], 1)

            def add_b2(m, j):
                m, j, _ = tile(m, j, TURNED)
                if j == 0:
                    pool.wait_ge(s["xc_made"], m + 1)
                pool.tensor_tensor(res[:, m, j, :], res[:, m, j, :], b2_all[:], ALU.add).then_inc(s["b2_added"], 1)

            pool.wait_ge(s["late_in"], LATE)
            pool.wait_ge(s["w_quantised"], 2)
            for n in (0, 1):
                out_im_products(n)
                out_im(n)
            out_im_products(2)
            out_im(2)
            x_rms(0)
            out_im_products(3)
            out_im(3)
            aug_parts(0)
            x_rms(1)
            aug_parts(1)
            x_rms(2)
            aug_parts(2)
            h_math(0, 0)
            x_rms(3)
            h_math(0, 1)
            aug_parts(3)
            h_math(0, 2)
            for m in (0, 1):
                for j in range(NA):
                    if NA * m + j >= TURNED:
                        h_math(m, j, others=True)
            with pool.Fori(2, NB) as m:
                for j in range(NA):
                    h_math(m, j, others=True)
            for j in range(TURNED):
                h_deq(NB, j)
                add_b2(NB, j)


def kernel(**inputs):
    import concourse.bacc as bacc
    from concourse.bass_utils import run_bass_kernel_spmd

    def given(name):
        return np.ascontiguousarray(inputs[name])

    def turned(name):
        return np.ascontiguousarray(np.asarray(inputs[name]).T)

    forward, to_signal, eye, parts = dft_constants()
    arrays = {
        "x": given("x"),
        "ctx": given("ctx_1024"),
        "wq_t": turned("L0_xattn_Wq"),
        "wkv_t": np.concatenate([turned("L0_xattn_Wk"), turned("L0_xattn_Wv")], axis=1),
        "wo_t": turned("L0_xattn_Wo"),
        "bq": given("L0_xattn_bq"),
        "bkv": np.concatenate([given("L0_xattn_bk"), given("L0_xattn_bv")]),
        "bo": given("L0_xattn_bo"),
        "w1_t": turned("L0_ffn_w1"),
        "b1": given("L0_ffn_b1"),
        "w2_t": turned("L0_ffn_w2"),
        "b2": given("L0_ffn_b2"),
        "c_forward": forward,
        "c_signal": to_signal,
        "c_eye": eye,
        "c_parts": parts,
    }
    nc = bacc.Bacc("TRN2", target_bir_lowering=False, num_devices=1)
    args = [nc.dram_tensor(f"in_{k}", a.shape, mybir.dt.from_np(a.dtype), kind="ExternalInput").ap() for k, a in arrays.items()]
    out = nc.dram_tensor("out", (NB, L, D), F32, kind="ExternalOutput").ap()
    build(nc, *args, out)
    r = run_bass_kernel_spmd(nc, [{f"in_{k}": a for k, a in arrays.items()}], core_ids=[0])
    return r.results[0]["out"]
```
